# Optimizing a Trainium2 kernel written in Bass

```python
import numpy as np
import jax
import jax.numpy as jnp

def _softmax(x, axis=-1):
    return jax.nn.softmax(x, axis=axis)

def _gelu(x):
    return jax.nn.gelu(x, approximate=True)

def _silu(x):
    return jax.nn.silu(x)

def _sigmoid(x):
    return jax.nn.sigmoid(x)

def _layernorm(x, axis=-1, eps=1e-05):
    m = jnp.mean(x, axis=axis, keepdims=True)
    v = jnp.var(x, axis=axis, keepdims=True)
    return (x - m) / jnp.sqrt(v + eps)

def _scatter_add(tgt, idx, src, axis=0):
    return tgt.at[idx].add(src)

def _segment_sum(src, seg, n):
    return jax.ops.segment_sum(src, seg, n)
kernel_name = 'mk_gnn_resnorm_d4_gnn_r8_a3efae'

def setup_inputs(seed: int=0):
    np.random.seed(seed)
    _w = jnp.asarray

    def _rec_inputs():
        import jax
        import jax.numpy as jnp
        _gk = jax.random.key(seed)
        x = -0.000202 + 1 * jax.random.normal(jax.random.fold_in(_gk, 1), (6250, 128), jnp.float32)
        _s = jax.random.randint(jax.random.fold_in(_gk, 2), (50000,), 0, 6250, jnp.int32)
        _d = jax.random.randint(jax.random.fold_in(_gk, 3), (50000,), 0, 6250, jnp.int32)
        _loop = jnp.arange(6250, dtype=jnp.int32)
        src = jnp.concatenate([_s, _d, _loop])
        dst = jnp.concatenate([_d, _s, _loop])
        _o = jnp.argsort(dst, stable=True)
        src = src[_o]
        dst = dst[_o]
        edge_attr_64 = 0.000167468 + 1.0002 * jax.random.normal(jax.random.fold_in(_gk, 11), (106250, 64), jnp.float32)
        edge_weight = jax.random.uniform(jax.random.fold_in(_gk, 13), (106250,), jnp.float32, 0.0, 0.999998)
        return (x, src, dst, edge_attr_64, edge_weight)
    x, src, dst, edge_attr_64, edge_weight = _rec_inputs()

    def _L0_gnn_setup():
        import jax, jax.numpy as jnp
        import numpy as np
        N_NODES = 6250
        N_EDGES = 80000
        NODE_DIM = 128
        EDGE_DIM = 64
        HIDDEN_DIM = 128
        key = jax.random.key(seed)
        ks = jax.random.split(key, 12)
        x = jax.random.normal(ks[0], (N_NODES, NODE_DIM), dtype=jnp.float32)
        edge_index = jax.random.randint(ks[1], (2, N_EDGES), 0, N_NODES, dtype=jnp.int64)
        edge_attr = jax.random.normal(ks[2], (N_EDGES, EDGE_DIM), dtype=jnp.float32)
        fan1 = NODE_DIM + EDGE_DIM
        W1 = jax.random.normal(ks[3], (HIDDEN_DIM, fan1), dtype=jnp.float32) / np.sqrt(fan1)
        b1 = jnp.zeros((HIDDEN_DIM,), dtype=jnp.float32)
        W2 = jax.random.normal(ks[4], (HIDDEN_DIM, HIDDEN_DIM), dtype=jnp.float32) / np.sqrt(HIDDEN_DIM)
        b2 = jnp.zeros((HIDDEN_DIM,), dtype=jnp.float32)
        Wih = jax.random.normal(ks[5], (3 * NODE_DIM, HIDDEN_DIM), dtype=jnp.float32) / np.sqrt(HIDDEN_DIM)
        bih = jnp.zeros((3 * NODE_DIM,), dtype=jnp.float32)
        Whh = jax.random.normal(ks[6], (3 * NODE_DIM, NODE_DIM), dtype=jnp.float32) / np.sqrt(NODE_DIM)
        bhh = jnp.zeros((3 * NODE_DIM,), dtype=jnp.float32)
        return {'x': x, 'edge_index': edge_index, 'edge_attr': edge_attr, 'W1': W1, 'b1': b1, 'W2': W2, 'b2': b2, 'Wih': Wih, 'bih': bih, 'Whh': Whh, 'bhh': bhh}
    _L0_gnn_all = _L0_gnn_setup()
    _L0_gnn_in = {k: v for k, v in _L0_gnn_all.items() if k in ('W1', 'b1', 'W2', 'b2', 'Wih', 'bih', 'Whh', 'bhh')}
    del _L0_gnn_all

    def _L1_gnn_setup():
        import jax, jax.numpy as jnp
        import numpy as np

        def _augment_edges(edge_index, num_nodes):
            src0, dst0 = (edge_index[0], edge_index[1])
            loop = jnp.arange(num_nodes, dtype=edge_index.dtype)
            src = jnp.concatenate([src0, dst0, loop])
            dst = jnp.concatenate([dst0, src0, loop])
            return (src, dst)
        key = jax.random.key(seed)
        k1, k2, k3 = jax.random.split(key, 3)
        N, E, D_IN, D_OUT = (12500, 125000, 128, 128)
        x = jax.random.normal(k1, (N, D_IN), dtype=jnp.float32)
        edge_index = jax.random.randint(k2, (2, E), 0, N, dtype=jnp.int64)
        W = jax.random.normal(k3, (D_OUT, D_IN), dtype=jnp.float32) * (1.0 / np.sqrt(D_IN))
        bias = jnp.zeros((D_OUT,), dtype=jnp.float32)
        return {'x': x, 'edge_index': edge_index, 'W': W, 'bias': bias, 'num_nodes': N}
    _L1_gnn_all = _L1_gnn_setup()
    _L1_gnn_in = {k: v for k, v in _L1_gnn_all.items() if k in ('W', 'bias')}
    del _L1_gnn_all

    def _L2_gnn_setup():
        import jax, jax.numpy as jnp
        import numpy as np
        N = 6250
        E = 100000
        D_IN = 128
        D_OUT = 128
        key = jax.random.key(seed)
        k1, k2, k3 = jax.random.split(key, 3)
        seq = jax.random.normal(k1, (N, D_IN), dtype=jnp.float32)
        edge_index = jax.random.randint(k2, (2, E), 0, N, dtype=jnp.int32)
        W = jax.random.normal(k3, (D_IN, D_OUT), dtype=jnp.float32) * (1.0 / np.sqrt(D_IN))
        b = jnp.zeros((D_OUT,), dtype=jnp.float32)
        prelu_w = jnp.full((1,), 0.25, dtype=jnp.float32)
        return {'seq': seq, 'edge_index': edge_index, 'W': W, 'b': b, 'prelu_w': prelu_w}
    _L2_gnn_all = _L2_gnn_setup()
    _L2_gnn_in = {k: v for k, v in _L2_gnn_all.items() if k in ('W', 'b', 'prelu_w')}
    del _L2_gnn_all

    def _L3_gnn_setup():
        import jax, jax.numpy as jnp
        import numpy as np
        N_NODES = 6250
        N_EDGES = 100000
        IN_C, HID, OUT_C = (128, 256, 128)

        def _gcn_norm(edge_index, edge_weight, n_nodes):
            loop = jnp.arange(n_nodes, dtype=edge_index.dtype)
            src = jnp.concatenate([edge_index[0], loop])
            dst = jnp.concatenate([edge_index[1], loop])
            w = jnp.concatenate([edge_weight, jnp.ones((n_nodes,), edge_weight.dtype)])
            deg = jax.ops.segment_sum(w, dst, num_segments=n_nodes)
            dinv = jnp.where(deg > 0, deg ** (-0.5), 0.0)
            norm = dinv[src] * w * dinv[dst]
            return (src, dst, norm)

        def _gcn_conv(x, W, b, src, dst, norm, n_nodes):
            m = x @ W
            msg = m[src] * norm[:, None]
            out = jax.ops.segment_sum(msg, dst, num_segments=n_nodes)
            return out + b
        key = jax.random.key(seed)
        ks = jax.random.split(key, 10)
        x = jax.random.normal(ks[0], (N_NODES, IN_C), dtype=jnp.float32)
        edge_index = jax.random.randint(ks[1], (2, N_EDGES), 0, N_NODES, dtype=jnp.int64)
        edge_weight = jax.random.uniform(ks[2], (N_EDGES,), dtype=jnp.float32)

        def glorot(k, fan_in, fan_out):
            lim = (6.0 / (fan_in + fan_out)) ** 0.5
            return jax.random.uniform(k, (fan_in, fan_out), minval=-lim, maxval=lim, dtype=jnp.float32)
        W1 = glorot(ks[3], IN_C, HID)
        b1 = jnp.zeros((HID,), jnp.float32)
        W2 = glorot(ks[4], HID, HID)
        b2 = jnp.zeros((HID,), jnp.float32)
        W3 = glorot(ks[5], HID, OUT_C)
        b3 = jnp.zeros((OUT_C,), jnp.float32)
        return {'x': x, 'edge_index': edge_index, 'edge_weight': edge_weight, 'W1': W1, 'b1': b1, 'W2': W2, 'b2': b2, 'W3': W3, 'b3': b3}
    _L3_gnn_all = _L3_gnn_setup()
    _L3_gnn_in = {k: v for k, v in _L3_gnn_all.items() if k in ('W1', 'b1', 'W2', 'b2', 'W3', 'b3')}
    del _L3_gnn_all
    return {'x': x, 'src': src, 'dst': dst, 'edge_attr_64': edge_attr_64, 'edge_weight': edge_weight, 'L0_gnn_W1': _L0_gnn_in['W1'], 'L0_gnn_b1': _L0_gnn_in['b1'], 'L0_gnn_W2': _L0_gnn_in['W2'], 'L0_gnn_b2': _L0_gnn_in['b2'], 'L0_gnn_Wih': _L0_gnn_in['Wih'], 'L0_gnn_bih': _L0_gnn_in['bih'], 'L0_gnn_Whh': _L0_gnn_in['Whh'], 'L0_gnn_bhh': _L0_gnn_in['bhh'], 'L1_gnn_W': _L1_gnn_in['W'], 'L1_gnn_bias': _L1_gnn_in['bias'], 'L2_gnn_W': _L2_gnn_in['W'], 'L2_gnn_b': _L2_gnn_in['b'], 'L2_gnn_prelu_w': _L2_gnn_in['prelu_w'], 'L3_gnn_W1': _L3_gnn_in['W1'], 'L3_gnn_b1': _L3_gnn_in['b1'], 'L3_gnn_W2': _L3_gnn_in['W2'], 'L3_gnn_b2': _L3_gnn_in['b2'], 'L3_gnn_W3': _L3_gnn_in['W3'], 'L3_gnn_b3': _L3_gnn_in['b3']}

def reference(x, src, dst, edge_attr_64, edge_weight, L0_gnn_W1, L0_gnn_b1, L0_gnn_W2, L0_gnn_b2, L0_gnn_Wih, L0_gnn_bih, L0_gnn_Whh, L0_gnn_bhh, L1_gnn_W, L1_gnn_bias, L2_gnn_W, L2_gnn_b, L2_gnn_prelu_w, L3_gnn_W1, L3_gnn_b1, L3_gnn_W2, L3_gnn_b2, L3_gnn_W3, L3_gnn_b3):
    import jax
    import jax.numpy as jnp

    def _L0_gnn_ref(x, edge_index, edge_attr, W1, b1, W2, b2, Wih, bih, Whh, bhh):
        import jax, jax.numpy as jnp
        import numpy as np
        N_NODES = 6250
        N_EDGES = 80000
        NODE_DIM = 128
        EDGE_DIM = 64
        HIDDEN_DIM = 128
        src, dst = (edge_index[0], edge_index[1])
        msg_in = jnp.concatenate([x[src], edge_attr], axis=-1)
        h = jax.nn.relu(msg_in @ W1.T + b1)
        messages = h @ W2.T + b2
        agg = jax.ops.segment_sum(messages, dst, num_segments=x.shape[0])
        gi = agg @ Wih.T + bih
        gh = x @ Whh.T + bhh
        i_r, i_z, i_n = jnp.split(gi, 3, axis=-1)
        h_r, h_z, h_n = jnp.split(gh, 3, axis=-1)
        r = jax.nn.sigmoid(i_r + h_r)
        z = jax.nn.sigmoid(i_z + h_z)
        n = jnp.tanh(i_n + r * h_n)
        return (1.0 - z) * n + z * x

    def _L1_gnn_ref(x, edge_index, W, bias, num_nodes):
        import jax, jax.numpy as jnp
        import numpy as np

        def _augment_edges(edge_index, num_nodes):
            src0, dst0 = (edge_index[0], edge_index[1])
            loop = jnp.arange(num_nodes, dtype=edge_index.dtype)
            src = jnp.concatenate([src0, dst0, loop])
            dst = jnp.concatenate([dst0, src0, loop])
            return (src, dst)
        src, dst = _augment_edges(edge_index, num_nodes)
        ones = jnp.ones(dst.shape[0], dtype=x.dtype)
        deg = jax.ops.segment_sum(ones, dst, num_segments=num_nodes)
        dis = jnp.where(deg > 0, jax.lax.rsqrt(jnp.maximum(deg, 1.0)), 0.0)
        norm = dis[src] * dis[dst]
        messages = x[src] * norm[:, None]
        agg = jax.ops.segment_sum(messages, dst, num_segments=num_nodes)
        out = agg @ W.T + bias
        return jax.nn.relu(out)

    def _L2_gnn_ref(seq, edge_index, W, b, prelu_w):
        import jax, jax.numpy as jnp
        import numpy as np
        N = 6250
        E = 100000
        D_IN = 128
        D_OUT = 128
        n = seq.shape[0]
        xW = seq @ W
        loop = jnp.arange(n, dtype=edge_index.dtype)
        row = jnp.concatenate([edge_index[0], loop])
        col = jnp.concatenate([edge_index[1], loop])
        deg = jax.ops.segment_sum(jnp.ones_like(col, dtype=xW.dtype), col, num_segments=n)
        dinv = jnp.where(deg > 0, jax.lax.rsqrt(deg), 0.0)
        norm = dinv[row] * dinv[col]
        msg = xW[row] * norm[:, None]
        out = jax.ops.segment_sum(msg, col, num_segments=n)
        out = out + b
        return jnp.where(out > 0, out, prelu_w[0] * out)

    def _L3_gnn_ref(x, edge_index, edge_weight, W1, b1, W2, b2, W3, b3):
        import jax, jax.numpy as jnp
        import numpy as np
        N_NODES = 6250
        N_EDGES = 100000
        IN_C, HID, OUT_C = (128, 256, 128)

        def _gcn_norm(edge_index, edge_weight, n_nodes):
            loop = jnp.arange(n_nodes, dtype=edge_index.dtype)
            src = jnp.concatenate([edge_index[0], loop])
            dst = jnp.concatenate([edge_index[1], loop])
            w = jnp.concatenate([edge_weight, jnp.ones((n_nodes,), edge_weight.dtype)])
            deg = jax.ops.segment_sum(w, dst, num_segments=n_nodes)
            dinv = jnp.where(deg > 0, deg ** (-0.5), 0.0)
            norm = dinv[src] * w * dinv[dst]
            return (src, dst, norm)

        def _gcn_conv(x, W, b, src, dst, norm, n_nodes):
            m = x @ W
            msg = m[src] * norm[:, None]
            out = jax.ops.segment_sum(msg, dst, num_segments=n_nodes)
            return out + b
        n = x.shape[0]
        src, dst, norm = _gcn_norm(edge_index, edge_weight, n)
        h = jax.nn.relu(_gcn_conv(x, W1, b1, src, dst, norm, n))
        h = jax.nn.relu(_gcn_conv(h, W2, b2, src, dst, norm, n))
        return _gcn_conv(h, W3, b3, src, dst, norm, n)
    edge_index = jnp.stack([src, dst])
    x = _layernorm(x + _L0_gnn_ref(x, edge_index, edge_attr_64, L0_gnn_W1, L0_gnn_b1, L0_gnn_W2, L0_gnn_b2, L0_gnn_Wih, L0_gnn_bih, L0_gnn_Whh, L0_gnn_bhh), axis=-1)
    x = _layernorm(x + _L1_gnn_ref(x, edge_index, L1_gnn_W, L1_gnn_bias, 6250), axis=-1)
    x = _layernorm(x + _L2_gnn_ref(x, edge_index, L2_gnn_W, L2_gnn_b, L2_gnn_prelu_w), axis=-1)
    x = _layernorm(x + _L3_gnn_ref(x, edge_index, edge_weight, L3_gnn_W1, L3_gnn_b1, L3_gnn_W2, L3_gnn_b2, L3_gnn_W3, L3_gnn_b3), axis=-1)
    return x

_drawn_inputs = setup_inputs


def setup_inputs(seed=0):
    import zlib

    import numpy as np

    out = dict(_drawn_inputs(seed))
    spreads = {'L0_gnn_b1': (0.0, 0.1),
     'L0_gnn_b2': (0.0, 0.1),
     'L0_gnn_bih': (0.0, 0.521),
     'L0_gnn_bhh': (0.0, 0.708),
     'L1_gnn_bias': (0.0, 0.1),
     'L2_gnn_b': (0.0, 0.1),
     'L3_gnn_b1': (0.0, 0.1),
     'L3_gnn_b2': (0.0, 0.1),
     'L3_gnn_b3': (0.0, 0.1)}
    factors = {'edge_weight': 3.372}
    for name, (base, spread) in spreads.items():
        noise = np.random.default_rng([zlib.crc32(name.encode()), seed]).standard_normal(out[name].shape)
        drawn = base * np.exp(spread * noise) if base else spread * noise
        out[name] = jnp.asarray(drawn.astype(out[name].dtype))
    for name, factor in factors.items():
        out[name] = (out[name] * factor).astype(out[name].dtype)
    return out
```

```python
from contextlib import ExitStack

import concourse.bass as bass
from concourse import mybir

P = 128
N = 6250
E = 106250
FD = 128
ED = 64
HID = 256
NB = (N + P - 1) // P
NP = NB * P
TH = 8
TS = 2 * TH
STEPS = -(-E // (P * TS))
T = STEPS * TS
TR = -(-T // P) * P
GSTEPS = -(-((T * P + NB * (P - 1)) // P) // TS)
GT = GSTEPS * TS
GTR = -(-GT // P) * P
W = 32
PAD_NODE = N
HOLE = 255.0
CB = 7
CHUNKS = NB // CB
EPS = 1e-5
assert CHUNKS * CB == NB and E <= T * P

F32 = mybir.dt.float32
BF16 = mybir.dt.bfloat16
I32 = mybir.dt.int32
U32 = mybir.dt.uint32
ALU = mybir.AluOpType
ACT = mybir.ActivationFunctionType
AX = mybir.AxisListType


def free_at_first(eng, *sems):
    for sem in sems:
        eng.sem_inc(sem, 1)


class Chain:

    def __init__(self, eng, sem):
        self.eng, self.sem, self.n = eng, sem, 0

    def step(self, ins):
        self.n += 1
        ins.then_inc(self.sem, 1)
        self.eng.wait_ge(self.sem, self.n)


def wait_apart(eng, sem, value, passed):
    eng.wait_ge(sem, value)
    eng.sem_inc(passed, 1)


def per_row(col, n):
    return col.unsqueeze(2).to_broadcast([col.shape[0], col.shape[1], n])


def per_block(row, k):
    return row.unsqueeze(1).to_broadcast([row.shape[0], k, row.shape[1]])


def build(nc, a, out):
    with ExitStack() as ctx:
        def sb(name, shape, dt=F32, c=ctx):
            return c.enter_context(nc.sbuf_tensor(name, shape, dt))

        phase_sems = []

        def sem(name):
            phase_sems.append(nc.alloc_semaphore(name=name))
            return phase_sems[-1]

        def clear_sems():
            nc.all_engine_barrier()
            nc.clear_and_free_semaphores(list(phase_sems))
            nc.all_engine_barrier()
            phase_sems.clear()

        p_table = nc.dram_tensor("p_table", [NP, FD], F32).ap()
        tables = [nc.dram_tensor(f"x_table{i}", [NP, FD], F32).ap() for i in range(3)]
        h_tables = [nc.dram_tensor(f"h_table{i}", [NP, HID], F32).ap() for i in range(2)]
        groups = nc.dram_tensor("groups", [GTR * P, 2], F32).ap()

        iota_row = sb("iota_row", [P, P])
        ident = sb("ident", [P, P])
        ones = sb("ones", [P, P])
        src_i = sb("src_i", [P, T], I32)
        dst_i = sb("dst_i", [P, T], I32)
        weight = sb("weight", [P, T])
        local0 = sb("local0", [P, T])
        local = sb("local", [P, T])
        first = sb("first", [1, TR])
        first0 = sb("first0", [1, TR])
        first_i = sb("first_i", [1, TR], I32)
        rounds_i = sb("rounds_i", [P, 1], I32)
        g_local = sb("g_local", [P, GTR])
        g_src_i = sb("g_src_i", [P, GTR], I32)
        g_first_i = sb("g_first_i", [1, GTR], I32)
        dis1 = sb("dis1", [P, NB])
        dis2 = sb("dis2", [P, NB])
        dis3 = sb("dis3", [P, NB])
        indeg = sb("indeg", [P, NB])
        wihT = sb("wihT", [P, 3 * FD])
        whhT = sb("whhT", [P, 3 * FD])
        w2 = sb("w2", [P, FD])
        b2r = sb("b2r", [P, P])
        w1xT = sb("w1xT", [P, FD])
        w1eT = sb("w1eT", [ED + 1, FD])
        l1w = sb("l1w", [P, FD])
        l2w = sb("l2w", [P, FD])
        l3w1 = sb("l3w1", [P, HID])
        l3w2 = sb("l3w2", [P, 2, HID])
        l3w3 = sb("l3w3", [P, 2, FD])
        biases = sb("biases", [P, 3 * FD + 2 * HID + 1])
        l1b, l2b, l3b3 = (biases[:, i * FD:(i + 1) * FD] for i in range(3))
        l3b1, l3b2 = (biases[:, 3 * FD + i * HID:3 * FD + (i + 1) * HID] for i in range(2))
        prelu = biases[:, 3 * FD + 2 * HID:3 * FD + 2 * HID + 1]
        gru_bias = sb("gru_bias", [1, 4 * FD])
        wcT = sb("wcT", [P, 3 * FD])
        bv = sb("bv", [P, 4 * FD])

        ring = sb("ring", [P, 2, TH, HID])
        idx_buf = sb("idx_buf", [P, 2, TH], I32)
        hot = sb("hot", [P, 2, TH, P])

        with ExitStack() as c:
            iota_i = sb("iota_i", [P, P], I32, c)
            row_i = sb("row_i", [P, 1], I32, c)
            row_f = sb("row_f", [P, 1], F32, c)
            rows_i = sb("rows_i", [P, TR // P, P], I32, c)
            rows_f = sb("rows_f", [P, TR // P, P], F32, c)
            lo = sb("lo", [P, TR // P], F32, c)
            hi = sb("hi", [P, TR // P], F32, c)
            diag = sb("diag", [P, 2, TR // P, P], F32, c)
            rep = sb("rep", [P, 2, TR], F32, c)
            span = sb("span", [P, T], F32, c)
            span_i = sb("span_i", [P, T], I32, c)
            span_m = sb("span_m", [P, 1], F32, c)
            ps_rep = c.enter_context(nc.psum_tensor("ps_rep", [P, 2, 1024], F32))
            ps_w = c.enter_context(nc.psum_tensor("ps_w", [P, 2, 512], F32))
            edges_in, rows_in, weights_in, iotas = sem("edges_in"), sem("rows_in"), sem("weights_in"), sem("iotas")
            a_dve, diags_done, rep_done, wmul_done = sem("a_dve"), sem("diags_done"), sem("rep_done"), sem("wmul_done")
            ones_done = sem("ones_done")
            with nc.Block() as block:
                @block.sync
                def _(sp):
                    sp.dma_start(rows_i[:], a["dst_rows"]).then_inc(rows_in, 16)
                    sp.dma_start(src_i[:], a["src_cols"]).then_inc(edges_in, 16)
                    sp.dma_start(dst_i[:], a["dst_cols"]).then_inc(edges_in, 16)
                    sp.dma_start(weight[:], a["w_cols"]).then_inc(edges_in, 16)
                    loads = [(wihT, "wihT"), (whhT, "whhT"), (w2, "w2"), (b2r, "b2r"), (w1xT, "w1xT"), (w1eT, "w1eT"),
                             (l1w, "l1w"), (l2w, "l2w"), (l3w1, "l3w1"), (l3w2, "l3w2"), (l3w3, "l3w3"),
                             (biases, "biases")]
                    for to, name in loads:
                        sp.dma_start(to[:], a[name]).then_inc(weights_in, 16)
                    sp.wait_ge(edges_in, 48)
                    sp.wait_ge(weights_in, 16 * len(loads))

                @block.gpsimd
                def _(pool):
                    nc.gpsimd.iota(iota_i[:], [[1, P]], base=0, channel_multiplier=0).then_inc(iotas, 1)
                    nc.gpsimd.iota(row_i[:], [[1, 1]], base=0, channel_multiplier=1).then_inc(iotas, 1)

                @block.vector
                def _(dve):
                    chain = Chain(dve, a_dve)
                    nc.vector.memset(ones[:], 1.0).then_inc(ones_done, 1)
                    dve.wait_ge(iotas, 2)
                    chain.step(nc.vector.tensor_copy(iota_row[:], iota_i[:]))
                    chain.step(nc.vector.tensor_copy(row_f[:], row_i[:]))
                    chain.step(nc.vector.tensor_scalar(ident[:], iota_row[:], row_f[:, 0:1], None, ALU.is_equal))
                    dve.wait_ge(rows_in, 16)
                    chain.step(nc.vector.tensor_copy(rows_f[:], rows_i[:]))
                    chain.step(nc.vector.tensor_reduce(lo[:], rows_f[:], AX.X, ALU.min))
                    chain.step(nc.vector.tensor_reduce(hi[:], rows_f[:], AX.X, ALU.max))
                    for q, v in enumerate((lo, hi)):
                        nc.vector.tensor_tensor(diag[:, q], per_block(ident[:], TR // P), per_row(v[:], P),
                                                ALU.mult).then_inc(diags_done, 1)
                    dve.wait_ge(rep_done, 1)
                    chain.step(nc.vector.tensor_copy(rep[:], ps_rep[:, :, 0:TR]))
                    dve.wait_ge(edges_in, 48)
                    chain.step(nc.vector.tensor_copy(span[:], dst_i[:]))
                    chain.step(nc.vector.tensor_tensor(local0[:], span[:], rep[:, 0, 0:T], ALU.subtract))
                    chain.step(nc.vector.tensor_copy(first0[:], rep[0:1, 0, :]))
                    chain.step(nc.vector.tensor_tensor(span[:], rep[:, 1, 0:T], rep[:, 0, 0:T], ALU.subtract))
                    chain.step(nc.vector.tensor_reduce(span_m[:], span[:], AX.X, ALU.max))
                    chain.step(nc.vector.tensor_copy(span_i[:, 0:1], span_m[:]))
                    chain.step(nc.vector.tensor_scalar(span_i[:, 1:2], span_i[:, 0:1], W.bit_length() - 1, None,
                                                       ALU.arith_shift_right))
                    chain.step(nc.vector.tensor_copy(span_m[:], span_i[:, 1:2]))
                    chain.step(nc.vector.tensor_scalar(span_m[:], span_m[:], 1.0, None, ALU.add))
                    chain.step(nc.vector.tensor_copy(rounds_i[:], span_m[:]))
                    dve.wait_ge(wmul_done, 1)
                    chain.step(nc.vector.tensor_copy(wcT[:], ps_w[:, 0, 0:3 * FD]))
                    chain.step(nc.vector.tensor_copy(bv[:, 0:3 * FD], ps_w[:, 1, 0:3 * FD]))
                    chain.step(nc.vector.memset(bv[:, 3 * FD:], 0.0))

                @block.tensor
                def _(pe):
                    pe.wait_ge(ones_done, 1)
                    pe.wait_ge(diags_done, 2)
                    for q in range(2):
                        for b in range(TR // P):
                            mm = nc.tensor.matmul(ps_rep[:, q, b * P:(b + 1) * P], ones[:], diag[:, q, b, :],
                                                  start=True, stop=True)
                    mm.then_inc(rep_done, 1)
                    pe.wait_ge(weights_in, 16 * 12)
                    nc.tensor.matmul(ps_w[:, 0, 0:3 * FD], w2[:], wihT[:], start=True, stop=True)
                    nc.tensor.matmul(ps_w[:, 1, 0:3 * FD], b2r[:], wihT[:], start=True, stop=True).then_inc(wmul_done, 1)

        with ExitStack() as c:
            src_blk = sb("src_blk", [P, T], F32, c)
            src_row = sb("src_row", [P, T], F32, c)
            dst_blk = sb("dst_blk", [P, T], F32, c)
            dst_row = sb("dst_row", [P, T], F32, c)
            place_i = sb("place_i", [P, T], I32, c)
            record = sb("record", [P, T, 2], F32, c)
            xT = sb("xT", [P, NP], F32, c)
            before_i = sb("before_i", [P, T], I32, c)
            with ExitStack() as c2:
                tri = sb("tri", [P, P], F32, c2)
                tri_b = sb("tri_b", [P, P], BF16, c2)
                ones_b = sb("ones_b", [P, 1], BF16, c2)
                holes = sb("holes", [P, GTR, 2], F32, c2)
                in_blk = sb("in_blk", [P, 2, TS, NB], BF16, c2)
                spread = sb("spread", [NB, 2, TH, NB], F32, c2)
                picked = sb("picked", [P, 2, TH, NB], F32, c2)
                place = sb("place", [P, T], F32, c2)
                count = sb("count", [NB, T], F32, c2)
                upto = sb("upto", [NB, T], F32, c2)
                pre = sb("pre", [NB, T], F32, c2)
                ones_t = sb("ones_t", [NB, T], F32, c2)
                size = sb("size", [NB, 4], F32, c2)
                size_i = sb("size_i", [NB, 3], I32, c2)
                col = sb("col", [P, 1], F32, c2)
                col_i = sb("col_i", [P, 1], I32, c2)
                tile_i = sb("tile_i", [NB, GTR], I32, c2)
                tile_f = sb("tile_f", [NB, GTR], F32, c2)
                ended = sb("ended", [NB, GTR], F32, c2)
                g_first = sb("g_first", [1, GTR], F32, c2)
                ps_cnt = c2.enter_context(nc.psum_tensor("ps_cnt", [P, 2, 512], F32))
                ps_pos = c2.enter_context(nc.psum_tensor("ps_pos", [P, 2, 512], F32))
                ps_map = c2.enter_context(nc.psum_tensor("ps_map", [P, 2, 512], F32))
                ps_base = c2.enter_context(nc.psum_tensor("ps_base", [P, 512], F32))
                b_dve, holes_out, holes_set, b_iota = sem("b_dve"), sem("holes_out"), sem("holes_set"), sem("b_iota")
                xt_in = sem("xt_in")
                blk_ready = [sem(f"blk_ready{h}") for h in range(2)]
                blk_counted = [sem(f"blk_counted{h}") for h in range(2)]
                counts_read = [sem(f"counts_read{h}") for h in range(2)]
                place_ready = [sem(f"place_ready{h}") for h in range(2)]
                place_mul = [sem(f"place_mul{h}") for h in range(2)]
                place_read = [sem(f"place_read{h}") for h in range(2)]
                pick_done = sem("pick_done")
                size_ready, base_done, ended_ready, map_done = sem("size_ready"), sem("base_done"), sem("ended_ready"), sem("map_done")
                PSTEPS = T // TS
                with nc.Block() as block:
                    @block.sync
                    def _(sp):
                        sp.dma_start(xT[:], a["x_feat"]).then_inc(xt_in, 16)
                        sp.wait_ge(holes_set, 2)
                        sp.dma_start(groups.rearrange("(p t) w -> p (t w)", p=P),
                                     holes[:].rearrange("p t w -> p (t w)")).then_inc(holes_out, 16)
                        sp.wait_ge(holes_out, 16)
                        sp.wait_ge(xt_in, 16)

                    @block.gpsimd
                    def _(pool):
                        nc.gpsimd.memset(holes[:, :, 0], HOLE).then_inc(holes_set, 1)
                        nc.gpsimd.memset(holes[:, :, 1], 0.0).then_inc(holes_set, 1)
                        nc.gpsimd.iota(tile_i[:], [[P, GTR]], base=0, channel_multiplier=0).then_inc(b_iota, 1)
                        nc.gpsimd.iota(col_i[:], [[1, 1]], base=0, channel_multiplier=1).then_inc(b_iota, 1)

                    @block.vector
                    def _(dve):
                        chain = Chain(dve, b_dve)
                        for idx, blk, row in ((src_i, src_blk, src_row), (dst_i, dst_blk, dst_row)):
                            chain.step(nc.vector.tensor_scalar(before_i[:], idx[:], 7, None, ALU.arith_shift_right))
                            chain.step(nc.vector.tensor_copy(blk[:], before_i[:]))
                            chain.step(nc.vector.tensor_scalar(before_i[:], idx[:], P - 1, None, ALU.bitwise_and))
                            chain.step(nc.vector.tensor_copy(row[:], before_i[:]))
                        chain.step(nc.vector.tensor_copy(record[:, :, 0], src_row[:]))
                        chain.step(nc.vector.tensor_copy(record[:, :, 1], dst_i[:]))
                        dve.wait_ge(b_iota, 2)
                        chain.step(nc.vector.tensor_copy(col[:], col_i[:]))
                        chain.step(nc.vector.tensor_copy(tile_f[:], tile_i[:]))
                        chain.step(nc.vector.tensor_scalar(tri[:], iota_row[:], col[:, 0:1], None, ALU.is_gt))
                        chain.step(nc.vector.tensor_copy(tri_b[:], tri[:]))
                        chain.step(nc.vector.memset(ones_b[:], 1.0))
                        chain.step(nc.vector.memset(ones_t[:], 1.0))
                        free_at_first(dve, *counts_read, *place_read)
                        with dve.Fori(0, PSTEPS // 2) as i:
                            for h in range(2):
                                t0 = i * (2 * TS) + h * TS
                                nc.vector.tensor_tensor(in_blk[:, h], per_block(iota_row[:, 0:NB], TS),
                                                        per_row(src_blk[:, bass.ds(t0, TS)], NB),
                                                        ALU.is_equal).then_inc(blk_ready[h], 1)
                            for h in range(2):
                                t0 = i * (2 * TS) + h * TS
                                dve.wait_ge(blk_counted[h], i + 1)
                                nc.vector.tensor_copy(count[:, bass.ds(t0, TS)],
                                                      ps_cnt[0:NB, h, 0:TS]).then_inc(counts_read[h], 1)
                        for h in range(2):
                            dve.wait_ge(counts_read[h], PSTEPS // 2 + 1)
                        chain.step(nc.vector.tensor_tensor_scan(upto[:], ones_t[:], count[:], 0.0, ALU.mult, ALU.add))
                        chain.step(nc.vector.tensor_scalar(size[:, 0:1], upto[:, T - 1:T], float(P - 1), None, ALU.add))
                        chain.step(nc.vector.tensor_copy(size_i[:, 0:1], size[:, 0:1]))
                        chain.step(nc.vector.tensor_scalar(size_i[:, 1:2], size_i[:, 0:1], -P, None, ALU.bitwise_and))
                        nc.vector.tensor_copy(size[:, 1:2], size_i[:, 1:2]).then_inc(size_ready, 1)
                        dve.wait_ge(size_ready, 1)
                        dve.wait_ge(base_done, 1)
                        chain.step(nc.vector.tensor_copy(size[:, 2:3], ps_base[0:NB, 0:1]))
                        chain.step(nc.vector.tensor_tensor(size[:, 3:4], size[:, 2:3], size[:, 1:2], ALU.add))
                        nc.vector.tensor_scalar(ended[:], tile_f[:], size[:, 3:4], None,
                                                ALU.is_ge).then_inc(ended_ready, 1)
                        chain.step(nc.vector.tensor_tensor(pre[:], upto[:], count[:], ALU.subtract))
                        chain.step(nc.vector.tensor_scalar(pre[:], pre[:], size[:, 2:3], None, ALU.add))
                        dve.wait_ge(map_done, 1)
                        for q in range(2):
                            chain.step(nc.vector.tensor_scalar(g_first[:, q * (GTR // 2):(q + 1) * (GTR // 2)],
                                                               ps_map[0:1, q, 0:GTR // 2], float(NB - 1), float(P),
                                                               ALU.min, ALU.mult))
                        chain.step(nc.vector.tensor_copy(g_first_i[:], g_first[:]))
                        with dve.Fori(0, PSTEPS) as i:
                            for h in range(2):
                                t0 = i * TS + h * TH
                                nc.vector.tensor_tensor(in_blk[:, h, 0:TH], per_block(iota_row[:, 0:NB], TH),
                                                        per_row(src_blk[:, bass.ds(t0, TH)], NB),
                                                        ALU.is_equal).then_inc(place_ready[h], 1)
                                nc.vector.tensor_tensor(spread[:, h], per_block(ident[0:NB, 0:NB], TH),
                                                        per_row(pre[:, bass.ds(t0, TH)], NB),
                                                        ALU.mult).then_inc(place_ready[h], 1)
                            for h in range(2):
                                t0 = i * TS + h * TH
                                dve.wait_ge(place_mul[h], i + 1)
                                nc.vector.tensor_tensor(picked[:, h], in_blk[:, h, 0:TH],
                                                        ps_pos[:, h, 0:TH * NB].rearrange("p (t b) -> p t b", b=NB),
                                                        ALU.mult).then_inc(pick_done, 1)
                                dve.wait_ge(pick_done, i * 2 + (h + 1))
                                nc.vector.tensor_reduce(place[:, bass.ds(t0, TH)], picked[:, h], AX.X,
                                                        ALU.add).then_inc(place_read[h], 1)
                        for h in range(2):
                            dve.wait_ge(place_read[h], PSTEPS + 1)
                        chain.step(nc.vector.tensor_copy(place_i[:], place[:]))

                    @block.tensor
                    def _(pe):
                        with pe.Fori(0, PSTEPS // 2) as i:
                            for h in range(2):
                                pe.wait_ge(blk_ready[h], i + 1)
                                pe.wait_ge(counts_read[h], i + 1)
                                for t in range(TS):
                                    mm = nc.tensor.matmul(ps_cnt[0:NB, h, t:t + 1], in_blk[:, h, t, :], ones_b[:],
                                                          start=True, stop=True)
                                mm.then_inc(blk_counted[h], 1)
                        pe.wait_ge(size_ready, 1)
                        nc.tensor.matmul(ps_base[0:NB, 0:1], tri[0:NB, 0:NB], size[:, 1:2], start=True,
                                         stop=True).then_inc(base_done, 1)
                        pe.wait_ge(ended_ready, 1)
                        for q in range(2):
                            mm = nc.tensor.matmul(ps_map[:, q, 0:GTR // 2], ones[0:NB, :],
                                                  ended[:, q * (GTR // 2):(q + 1) * (GTR // 2)], start=True, stop=True)
                        mm.then_inc(map_done, 1)
                        with pe.Fori(0, PSTEPS) as i:
                            for h in range(2):
                                pe.wait_ge(place_ready[h], i * 2 + 2)
                                pe.wait_ge(place_read[h], i + 1)
                                nc.tensor.matmul(ps_pos[:, h, 0:TH * NB], tri_b[:],
                                                 in_blk[:, h, 0:TH].rearrange("p t b -> p (t b)"), start=True, stop=False)
                                nc.tensor.matmul(ps_pos[:, h, 0:TH * NB], ones[0:NB, :],
                                                 spread[:, h].rearrange("p t b -> p (t b)"), start=False,
                                                 stop=True).then_inc(place_mul[h], 1)

            with ExitStack() as c2:
                rec_buf = sb("rec_buf", [P, 2, TH, 2], F32, c2)
                deg_src = sb("deg_src", [P, 2, TH, P], BF16, c2)
                deg_dst = sb("deg_dst", [P, 2, TH, 2, P], F32, c2)
                blk_src = sb("blk_src", [P, 2, TH, NB], BF16, c2)
                blk_dst = sb("blk_dst", [P, 2, TH, NB], F32, c2)
                deg_t = sb("deg_t", [NB, 3, P], F32, c2)
                deg = sb("deg", [P, 4, NB], F32, c2)
                zero = sb("zero", [P, 2 * P], F32, c2)
                p_sb = sb("p_sb", [P, NB, FD], F32, c2)
                ps_src = c2.enter_context(nc.psum_tensor("ps_src", [P, 512], F32))
                ps_dst = c2.enter_context(nc.psum_tensor("ps_dst", [P, 512], F32))
                ps_deg = c2.enter_context(nc.psum_tensor("ps_deg", [P, 512], F32))
                ps_p = c2.enter_context(nc.psum_tensor("ps_p", [P, 2, 512], F32))
                put = [sem(f"put{h}") for h in range(2)]
                put_ready = [sem(f"put_ready{h}") for h in range(2)]
                c_dve, c_pe, deg_eq = sem("c_dve"), sem("c_pe"), sem("deg_eq")
                hots_ready = [sem(f"hots_ready{h}") for h in range(2)]
                hots_used = [sem(f"hots_used{h}") for h in range(2)]
                deg_done, degt_ready, degT_done = sem("deg_done"), sem("degt_ready"), sem("degT_done")
                zero_set, deg_cleared = sem("zero_set"), sem("deg_cleared")
                p_mul, p_read, p_out, root_in, root_out = sem("p_mul"), sem("p_read"), sem("p_out"), sem("root_in"), sem("root_out")
                passed = sem("passed_put")
                PG = [(j, min(4, NB - j)) for j in range(0, NB, 4)]
                with nc.Block() as block:
                    @block.gpsimd
                    def _(pool):
                        with pool.Fori(0, STEPS) as i:
                            for h in range(2):
                                wait_apart(pool, put_ready[h], i * 2 + 2, passed)
                                for t in range(TH):
                                    pool.indirect_dma_start(
                                        groups, bass.IndirectOffsetOnAxis(idx_buf[:, h, t:t + 1].bitcast(U32), 0),
                                        rec_buf[:, h, t, :], None).then_inc(put[h], 16)
                        for h in range(2):
                            pool.wait_ge(put[h], 16 * TH * STEPS)

                    @block.scalar
                    def _(act):
                        def fill(i, h):
                            t0 = i * TS + h * TH
                            nc.scalar.copy(idx_buf[:, h, :], place_i[:, bass.ds(t0, TH)]).then_inc(put_ready[h], 1)
                            nc.scalar.copy(rec_buf[:, h], record[:, bass.ds(t0, TH), :]).then_inc(put_ready[h], 1)

                        for h in range(2):
                            fill(0, h)
                        with act.Fori(1, STEPS) as i:
                            for h in range(2):
                                act.wait_ge(put[h], i * (16 * TH))
                                fill(i, h)
                        act.wait_ge(root_in, 1)
                        nc.scalar.activation(deg[:, 0:3, :], deg[:, 0:3, :], ACT.Sqrt).then_inc(root_out, 1)

                    @block.sync
                    def _(sp):
                        sp.wait_ge(p_read, len(PG))
                        sp.dma_start(p_table.rearrange("(b p) f -> p b f", p=P), p_sb[:]).then_inc(p_out, 16)
                        sp.wait_ge(p_out, 16)

                    @block.vector
                    def _(dve):
                        chain = Chain(dve, c_dve)
                        for q, (j, n) in enumerate(PG):
                            dve.wait_ge(p_mul, q + 1)
                            nc.vector.tensor_copy(p_sb[:, j:j + n, :], ps_p[:, q % 2, 0:n * FD].rearrange(
                                "p (b f) -> p b f", f=FD)).then_inc(p_read, 1)
                        nc.vector.memset(zero[:], 0.0).then_inc(zero_set, 1)
                        dve.wait_ge(zero_set, 1)
                        with dve.Fori(0, STEPS) as i:
                            for h in range(2):
                                t0 = i * TS + h * TH
                                dve.wait_ge(hots_used[h], i + 1)
                                nc.vector.tensor_tensor(deg_src[:, h], per_block(iota_row[:], TH),
                                                        per_row(src_row[:, bass.ds(t0, TH)], P),
                                                        ALU.is_equal).then_inc(hots_ready[h], 1)
                                nc.vector.tensor_tensor(blk_src[:, h], per_block(iota_row[:, 0:NB], TH),
                                                        per_row(src_blk[:, bass.ds(t0, TH)], NB),
                                                        ALU.is_equal).then_inc(hots_ready[h], 1)
                                nc.vector.tensor_tensor(blk_dst[:, h], per_block(iota_row[:, 0:NB], TH),
                                                        per_row(dst_blk[:, bass.ds(t0, TH)], NB),
                                                        ALU.is_equal).then_inc(hots_ready[h], 1)
                                nc.vector.tensor_tensor(deg_dst[:, h, :, 0, :], per_block(iota_row[:], TH),
                                                        per_row(dst_row[:, bass.ds(t0, TH)], P),
                                                        ALU.is_equal).then_inc(deg_eq, 1)
                                dve.wait_ge(deg_eq, i * 2 + (h + 1))
                                nc.vector.tensor_tensor(deg_dst[:, h, :, 1, :], deg_dst[:, h, :, 0, :],
                                                        per_row(weight[:, bass.ds(t0, TH)], P),
                                                        ALU.mult).then_inc(hots_ready[h], 1)
                        dve.wait_ge(deg_done, 1)
                        nc.vector.tensor_copy(deg_t[:, 0, :], ps_src[0:NB, 0:P]).then_inc(degt_ready, 1)
                        nc.vector.tensor_copy(deg_t[:, 1:3, :], ps_dst[0:NB, 0:2 * P].rearrange(
                            "b (q r) -> b q r", r=P)).then_inc(degt_ready, 1)
                        dve.wait_ge(degT_done, 1)
                        chain.step(nc.vector.tensor_copy(indeg[:], ps_deg[:, NB:2 * NB]))
                        chain.step(nc.vector.tensor_scalar(deg[:, 1, :], indeg[:], 1.0, None, ALU.add))
                        chain.step(nc.vector.tensor_tensor(deg[:, 0, :], deg[:, 1, :], ps_deg[:, 0:NB], ALU.add))
                        chain.step(nc.vector.tensor_scalar(deg[:, 2, :], ps_deg[:, 2 * NB:3 * NB], 1.0, None, ALU.add))
                        chain.step(nc.vector.tensor_scalar(deg[:, 3, :], deg[:, 2, :], 0.0, None, ALU.is_gt))
                        chain.step(nc.vector.tensor_scalar(deg[:, 0:2, :], deg[:, 0:2, :], 1.0, None, ALU.max))
                        nc.vector.tensor_scalar(deg[:, 2, :], deg[:, 2, :], 1e-30, None, ALU.max).then_inc(root_in, 1)
                        dve.wait_ge(root_out, 1)
                        chain.step(nc.vector.reciprocal(dis1[:], deg[:, 0, :]))
                        chain.step(nc.vector.reciprocal(dis2[:], deg[:, 1, :]))
                        chain.step(nc.vector.reciprocal(dis3[:], deg[:, 2, :]))
                        chain.step(nc.vector.tensor_tensor(dis3[:], dis3[:], deg[:, 3, :], ALU.mult))

                    @block.tensor
                    def _(pe):
                        for q, (j, n) in enumerate(PG):
                            if q >= 2:
                                pe.wait_ge(p_read, q - 1)
                            for b in range(n):
                                mm = nc.tensor.matmul(ps_p[:, q % 2, b * FD:(b + 1) * FD],
                                                      xT[:, (j + b) * P:(j + b + 1) * P], w1xT[:], start=True, stop=True)
                            mm.then_inc(p_mul, 1)
                        free_at_first(pe, *hots_used)
                        pe.wait_ge(zero_set, 1)
                        nc.tensor.matmul(ps_src[0:NB, 0:P], zero[:, 0:NB], zero[:, 0:P], start=True, stop=False)
                        nc.tensor.matmul(ps_dst[0:NB, 0:2 * P], zero[:, 0:NB], zero[:], start=True, stop=False)
                        with pe.Fori(0, STEPS) as i:
                            for h in range(2):
                                pe.wait_ge(hots_ready[h], i * 4 + 4)
                                for t in range(TH):
                                    nc.tensor.matmul(ps_src[0:NB, 0:P], blk_src[:, h, t, :], deg_src[:, h, t, :],
                                                     start=False, stop=False)
                                    mm = nc.tensor.matmul(ps_dst[0:NB, 0:2 * P], blk_dst[:, h, t, :],
                                                          deg_dst[:, h, t].rearrange("p q r -> p (q r)"),
                                                          start=False, stop=False)
                                mm.then_inc(hots_used[h], 1)
                        nc.tensor.matmul(ps_src[0:NB, 0:P], zero[:, 0:NB], zero[:, 0:P], start=False, stop=True)
                        nc.tensor.matmul(ps_dst[0:NB, 0:2 * P], zero[:, 0:NB], zero[:], start=False, stop=True).then_inc(deg_done, 1)
                        pe.wait_ge(degt_ready, 2)
                        for q in range(3):
                            mm = nc.tensor.transpose(ps_deg[:, q * NB:(q + 1) * NB], deg_t[:, q, :], ident[0:NB, 0:NB])
                        mm.then_inc(degT_done, 1)

        clear_sems()
        x = sb("x", [P, NB, FD])
        acc = sb("acc", [P, 2, NP + W])

        def sparse_pass(name, table, F, idx, local_src, first_src, steps, win, weights=None, rounds=True,
                        messages=None):
            K = F // P
            with ExitStack() as c:
                pa = c.enter_context(nc.psum_tensor(f"pa_{name}", [P, 2, max(512, TH * K * win)], F32))
                if messages:
                    edge = sb(f"edge_{name}", [ED + 1, 2, TH * P], F32, c)
                    msg = sb(f"msg_{name}", [P, 2, TH, FD], F32, c)
                    pm = c.enter_context(nc.psum_tensor(f"pm_{name}", [P, 2, TH * FD], F32))
                gathered = [sem(f"gathered_{name}{h}") for h in range(2)]
                idx_ready = [sem(f"idx_ready_{name}{h}") for h in range(2)]
                hot_ready = [sem(f"hot_ready_{name}{h}") for h in range(2)]
                summed = [sem(f"summed_{name}{h}") for h in range(2)]
                added = [sem(f"added_{name}{h}") for h in range(2)]
                add_chain, eq_done, round_set = sem(f"add_chain_{name}"), sem(f"eq_done_{name}"), sem(f"round_set_{name}")
                passed, passed_dve = sem(f"passed_{name}"), sem(f"passed_dve_{name}")
                if messages:
                    edge_in = [sem(f"edge_in_{name}{h}") for h in range(2)]
                    pre_done = [sem(f"pre_done_{name}{h}") for h in range(2)]
                    msg_done = [sem(f"msg_done_{name}{h}") for h in range(2)]

                def loops(eng, body):
                    if rounds:
                        n = eng.value_load(rounds_i[0:1, 0:1], min_val=1, max_val=NP // W)
                        with eng.Fori(0, n) as v:
                            body(v)
                    else:
                        body(0)

                with nc.Block() as block:
                    @block.gpsimd
                    def _(pool):
                        def a_round(v):
                            with pool.Fori(0, steps) as i:
                                done = v * steps + i
                                for h in range(2):
                                    wait_apart(pool, idx_ready[h], done + 1, passed)
                                    for t in range(TH):
                                        pool.indirect_dma_start(
                                            ring[:, h, t, 0:F], None, table,
                                            bass.IndirectOffsetOnAxis(idx_buf[:, h, t:t + 1].bitcast(U32), 0)
                                        ).then_inc(gathered[h], 16)
                        loops(pool, a_round)

                    @block.scalar
                    def _(act):
                        def copy_idx(done, i, h):
                            act.wait_ge(summed[h], done + 1)
                            nc.scalar.copy(idx_buf[:, h, :], idx[:, bass.ds(i * TS + h * TH, TH)]
                                           ).then_inc(idx_ready[h], 1)

                        def relu(done, h):
                            act.wait_ge(pre_done[h], done + 2)
                            for q in range(2):
                                r = nc.scalar.activation(
                                    msg[:, h, q * (TH // 2):(q + 1) * (TH // 2), :].rearrange("p t f -> p (t f)"),
                                    pm[:, h, q * 512:(q + 1) * 512], ACT.Relu)
                            r.then_inc(msg_done[h], 1)

                        def a_round(v):
                            if not messages:
                                with act.Fori(0, steps) as i:
                                    for h in range(2):
                                        copy_idx(v * steps + i, i, h)
                                return
                            for h in range(2):
                                copy_idx(v * steps, 0, h)
                            with act.Fori(0, steps - 1) as i:
                                for h in range(2):
                                    relu(v * steps + i, h)
                                    copy_idx(v * steps + i + 1, i + 1, h)
                            for h in range(2):
                                relu(v * steps + (steps - 1), h)
                        loops(act, a_round)

                    if messages:
                        @block.sync
                        def _(sp):
                            def a_round(v):
                                with sp.Fori(0, steps) as i:
                                    done = v * steps + i
                                    for h in range(2):
                                        sp.wait_ge(pre_done[h], done + 1)
                                        sp.dma_start(edge[:, h, :], messages[:, bass.ds((i * TS + h * TH) * P, TH * P)]
                                                     ).then_inc(edge_in[h], 16)
                            loops(sp, a_round)

                    @block.tensor
                    def _(pe):
                        free_at_first(pe, *summed, *(pre_done if messages else []))

                        def a_round(v):
                            with pe.Fori(0, steps) as i:
                                done = v * steps + i
                                for h in range(2):
                                    rows = ring
                                    if messages:
                                        pe.wait_ge(edge_in[h], done * 16 + 16)
                                        pe.wait_ge(gathered[h], done * (16 * TH) + 16 * TH)
                                        for t in range(TH):
                                            nc.tensor.matmul(pm[:, h, t * FD:(t + 1) * FD], edge[:, h, t * P:(t + 1) * P],
                                                             w1eT[:], start=True, stop=False)
                                            mm = nc.tensor.matmul(pm[:, h, t * FD:(t + 1) * FD], ident[:],
                                                                  ring[:, h, t, 0:FD], start=False, stop=True)
                                        mm.then_inc(pre_done[h], 1)
                                        pe.wait_ge(msg_done[h], done + 1)
                                        rows = msg
                                    else:
                                        pe.wait_ge(gathered[h], done * (16 * TH) + 16 * TH)
                                    pe.wait_ge(hot_ready[h], done + 1)
                                    pe.wait_ge(added[h], done + 1)
                                    for t in range(TH):
                                        for k in range(K):
                                            at = (t * K + k) * win
                                            mm = nc.tensor.matmul(pa[:, h, at:at + win], rows[:, h, t, k * P:(k + 1) * P],
                                                                  hot[:, h, t, 0:win], start=True, stop=True)
                                    mm.then_inc(summed[h], 1)
                        loops(pe, a_round)

                    @block.vector
                    def _(dve):
                        free_at_first(dve, *added)
                        setup = 0
                        if rounds:
                            nc.vector.tensor_scalar(local[:], local0[:], float(W), None, ALU.add).then_inc(round_set, 1)
                            nc.vector.tensor_scalar(first[:], first0[:], float(-W), None, ALU.add).then_inc(round_set, 1)
                            setup = 2
                            if messages:
                                nc.vector.memset(acc[:], 0.0).then_inc(round_set, 1)
                                setup = 3

                        def a_round(v):
                            if rounds:
                                dve.wait_ge(round_set, v * 3 + setup)
                                nc.vector.tensor_scalar(local[:], local[:], float(-W), None, ALU.add
                                                        ).then_inc(round_set, 1)
                                nc.vector.tensor_scalar(first[:], first[:], float(W), float(NP), ALU.add, ALU.min
                                                        ).then_inc(round_set, 1)
                                dve.wait_ge(round_set, v * 3 + setup + 2)
                                nc.vector.tensor_copy(first_i[:], first[:]).then_inc(round_set, 1)
                                wait_apart(dve, round_set, v * 3 + setup + 3, passed_dve)
                            with dve.Fori(0, steps) as i:
                                done = v * steps + i
                                for h in range(2):
                                    t0 = i * TS + h * TH
                                    eq = nc.vector.tensor_tensor(hot[:, h, :, 0:win], per_block(iota_row[:, 0:win], TH),
                                                                 per_row(local_src[:, bass.ds(t0, TH)], win), ALU.is_equal)
                                    if weights is None:
                                        eq.then_inc(hot_ready[h], 1)
                                    else:
                                        eq.then_inc(eq_done, 1)
                                        dve.wait_ge(eq_done, done * 2 + (h + 1))
                                        nc.vector.tensor_tensor(hot[:, h, :, 0:win], hot[:, h, :, 0:win],
                                                                per_row(weights[:, bass.ds(t0, TH)], win),
                                                                ALU.mult).then_inc(hot_ready[h], 1)
                                for h in range(2):
                                    t0 = i * TS + h * TH
                                    ats = [dve.value_load(first_src[0:1, bass.ds(t0 + t, 1)], min_val=0, max_val=NP + W - win)
                                           for t in range(TH)]
                                    dve.wait_ge(summed[h], done + 2)
                                    dve.wait_ge(added[1 - h], done + h + 1)
                                    for t in range(TH):
                                        to = acc[:, 0:K, bass.ds(ats[t], win)]
                                        add = nc.vector.tensor_tensor(
                                            to, to, pa[:, h, t * K * win:(t + 1) * K * win].rearrange(
                                                "p (k n) -> p k n", k=K), ALU.add)
                                        if t < TH - 1:
                                            add.then_inc(add_chain, 1)
                                            dve.wait_ge(add_chain, done * (2 * TH - 2) + (h * (TH - 1) + t + 1))
                                        else:
                                            add.then_inc(added[h], 1)
                        loops(dve, a_round)

        def dense(name, F, weights, kind, dis_in, bias, dis_out, table, last=False, xT=None):
            Kn = F // P
            with ExitStack() as c:
                width = 4 * FD if kind == "gru" else F
                y = sb(f"y_{name}", [P, CB, F], F32, c)
                t1 = sb(f"t1_{name}", [P, CB, width], F32, c)
                small = sb(f"small_{name}", [P, 4, CB], F32, c)
                nbuf = 2 if kind == "gru" else 1
                po = c.enter_context(nc.psum_tensor(f"po_{name}", [P, nbuf, CB * F if kind != "gru" else 512], F32))
                pt = c.enter_context(nc.psum_tensor(f"pt_{name}", [P, 2, 512], F32))
                conv_done, conv_read, d_dve = sem(f"conv_done_{name}"), sem(f"conv_read_{name}"), sem(f"d_dve_{name}")
                act_in, act_out, rows_ready = sem(f"act_in_{name}"), sem(f"act_out_{name}"), sem(f"rows_ready_{name}")
                rows_out, turned, turned_read = sem(f"rows_out_{name}"), sem(f"turned_{name}"), sem(f"turned_read_{name}")
                TP = [(k, q, min(4, CB - q)) for k in range(Kn) for q in range(0, CB, 4)]
                rows = y if not last else None

                with nc.Block() as block:
                    @block.tensor
                    def _(pe):
                        for ch in range(CHUNKS):
                            for b in range(CB):
                                j = ch * CB + b
                                s = slice(j * P, (j + 1) * P)
                                if kind == "gru":
                                    n = ch * CB + b
                                    if n >= 2:
                                        pe.wait_ge(conv_read, n - 1)
                                    o = po[:, n % 2, :]
                                    for cols, terms in (
                                            (slice(0, 2 * FD), [(xT[:, s], whhT[:, 0:2 * FD]),
                                                                (acc[:, 0, s], wcT[:, 0:2 * FD])]),
                                            (slice(2 * FD, 3 * FD), [(acc[:, 0, s], wcT[:, 2 * FD:])]),
                                            (slice(3 * FD, 4 * FD), [(xT[:, s], whhT[:, 2 * FD:])])):
                                        nc.tensor.matmul(o[:, cols], ones[0:1, :], gru_bias[:, cols],
                                                         start=True, stop=False)
                                        for q, (node_part, w) in enumerate(terms):
                                            mm = nc.tensor.matmul(o[:, cols], node_part, w, start=False,
                                                                  stop=(q == len(terms) - 1))
                                    mm.then_inc(conv_done, 1)
                                else:
                                    if ch and b == 0:
                                        pe.wait_ge(conv_read, ch)
                                    for q, (w, k) in enumerate(weights):
                                        mm = nc.tensor.matmul(po[:, 0, b * F:(b + 1) * F], acc[:, k, s], w,
                                                              start=(q == 0), stop=(q == len(weights) - 1))
                            if kind != "gru":
                                mm.then_inc(conv_done, 1)
                            if not last:
                                pe.wait_ge(rows_ready, ch + 1)
                                for q, (k, b0, n) in enumerate(TP):
                                    m = ch * len(TP) + q
                                    if m >= 2:
                                        pe.wait_ge(turned_read, m - 1)
                                    for b in range(n):
                                        mm = nc.tensor.transpose(pt[:, m % 2, b * P:(b + 1) * P],
                                                                 y[:, b0 + b, k * P:(k + 1) * P], ident[:])
                                    mm.then_inc(turned, 1)

                    @block.scalar
                    def _(act):
                        n_in = 0
                        for ch in range(CHUNKS):
                            def ask(fn):
                                nonlocal n_in
                                n_in += 1
                                act.wait_ge(act_in, n_in)
                                fn().then_inc(act_out, 1)
                            if kind == "gru":
                                ask(lambda: nc.scalar.activation(t1[:, :, 0:2 * FD], t1[:, :, 0:2 * FD], ACT.Sigmoid))
                                ask(lambda: nc.scalar.activation(t1[:, :, 2 * FD:3 * FD], t1[:, :, 2 * FD:3 * FD], ACT.Tanh))
                            if kind != "hidden":
                                ask(lambda: nc.scalar.activation(t1[:, :, 0:FD], y[:], ACT.Square))
                                ask(lambda: nc.scalar.activation(small[:, 2, :], small[:, 1, :], ACT.Sqrt))
                            if not last:
                                for q, (k, b0, n) in enumerate(TP):
                                    act.wait_ge(turned, ch * len(TP) + q + 1)
                                    nc.scalar.copy(acc[:, k, (ch * CB + b0) * P:(ch * CB + b0 + n) * P],
                                                   pt[:, (ch * len(TP) + q) % 2, 0:n * P]).then_inc(turned_read, 1)

                    @block.sync
                    def _(sp):
                        for ch in range(CHUNKS):
                            js = slice(ch * CB, (ch + 1) * CB)
                            sp.wait_ge(rows_ready, ch + 1)
                            if not last:
                                sp.dma_start(table.rearrange("(b p) f -> p b f", p=P)[:, js, :], y[:]
                                             ).then_inc(rows_out, 16)
                            elif ch < CHUNKS - 1:
                                sp.dma_start(out[ch * CB * P:(ch + 1) * CB * P, :].rearrange("(b p) f -> p b f", p=P),
                                             x[:, js, :]).then_inc(rows_out, 16)
                            else:
                                full = N // P
                                sp.dma_start(out[ch * CB * P:full * P, :].rearrange("(b p) f -> p b f", p=P),
                                             x[:, ch * CB:full, :]).then_inc(rows_out, 16)
                                sp.dma_start(out[full * P:N, :], x[0:N - full * P, full, :]).then_inc(rows_out, 16)
                        sp.wait_ge(rows_out, 16 * (CHUNKS + last))

                    @block.vector
                    def _(dve):
                        chain = Chain(dve, d_dve)
                        n_ask = 0

                        def ask(ins):
                            nonlocal n_ask
                            n_ask += 1
                            ins.then_inc(act_in, 1)
                            dve.wait_ge(act_out, n_ask)

                        V = nc.vector
                        for ch in range(CHUNKS):
                            js = slice(ch * CB, (ch + 1) * CB)
                            xc = x[:, js, :]
                            if ch and not last:
                                dve.wait_ge(rows_out, 16 * ch)
                                dve.wait_ge(turned, ch * len(TP))
                            if ch and last:
                                dve.wait_ge(rows_ready, ch)
                            if kind == "gru":
                                for b in range(CB):
                                    n = ch * CB + b
                                    dve.wait_ge(conv_done, n + 1)
                                    V.scalar_tensor_tensor(out=t1[:, b, :], in0=bv[:], scalar=indeg[:, n:n + 1],
                                                           in1=po[:, n % 2, :], op0=ALU.mult, op1=ALU.add
                                                           ).then_inc(conv_read, 1)
                                dve.wait_ge(conv_read, (ch + 1) * CB)
                                r, z, i_n, h_n = (t1[:, :, q * FD:(q + 1) * FD] for q in range(4))
                                n_ask += 1
                                chain.step(V.tensor_copy(small[:, 0, :], dis_out[:, js]))
                                V.tensor_copy(small[:, 1, :], dis_out[:, js]).then_inc(act_in, 1)
                                dve.wait_ge(act_out, n_ask)
                                chain.step(V.tensor_tensor(h_n, h_n, r, ALU.mult))
                                ask(V.tensor_tensor(i_n, i_n, h_n, ALU.add))
                                chain.step(V.tensor_tensor(h_n, xc, i_n, ALU.subtract))
                                chain.step(V.tensor_tensor(h_n, h_n, z, ALU.mult))
                                chain.step(V.tensor_tensor(h_n, h_n, i_n, ALU.add))
                                chain.step(V.tensor_tensor(y[:], h_n, xc, ALU.add))
                            else:
                                dve.wait_ge(conv_done, ch + 1)
                                V.tensor_tensor(y[:], po[:, 0, :].rearrange("p (b f) -> p b f", f=F),
                                                per_row(dis_in[:, js], F), ALU.mult).then_inc(conv_read, 1)
                                dve.wait_ge(conv_read, ch + 1)
                                chain.step(V.tensor_tensor(y[:], y[:], per_block(bias, CB), ALU.add))
                                if kind in ("relu", "hidden"):
                                    chain.step(V.tensor_scalar(y[:], y[:], 0.0, None, ALU.max))
                                if kind == "prelu":
                                    chain.step(V.tensor_scalar(t1[:], y[:], 0.0, prelu, ALU.min, ALU.mult))
                                    chain.step(V.scalar_tensor_tensor(out=y[:], in0=y[:], scalar=0.0, in1=t1[:],
                                                                      op0=ALU.max, op1=ALU.add))
                                if kind != "hidden":
                                    chain.step(V.tensor_tensor(y[:], y[:], xc, ALU.add))
                            if kind != "hidden":
                                s_sum, s_var, s_root, s_inv = (small[:, q, :] for q in range(4))
                                chain.step(V.tensor_reduce(s_sum, y[:], AX.X, ALU.add))
                                chain.step(V.tensor_scalar(s_sum, s_sum, 1.0 / FD, None, ALU.mult))
                                ask(V.tensor_tensor(y[:], y[:], per_row(s_sum, FD), ALU.subtract))
                                chain.step(V.tensor_reduce(s_var, t1[:, :, 0:FD], AX.X, ALU.add))
                                ask(V.tensor_scalar(s_var, s_var, 1.0 / FD, EPS, ALU.mult, ALU.add))
                                chain.step(V.reciprocal(s_inv, s_root))
                                norm = V.tensor_tensor(xc, y[:], per_row(s_inv, FD), ALU.mult)
                                if last:
                                    norm.then_inc(rows_ready, 1)
                                else:
                                    chain.step(norm)
                            if not last:
                                V.tensor_tensor(y[:], y[:] if kind == "hidden" else xc, per_row(dis_out[:, js], F),
                                                ALU.mult).then_inc(rows_ready, 1)

        sparse_pass("l0", p_table, FD, src_i, local, first_i, STEPS, W, messages=a["edge_feat"])
        with ExitStack() as c:
            xT2 = sb("xT2", [P, NP], F32, c)
            gb = sb("gb", [1, 3 * FD], F32, c)
            again_in, gb_done = sem("again_in"), sem("gb_done")
            with nc.Block() as block:
                @block.sync
                def _(sp):
                    sp.dma_start(xT2[:], a["x_feat"]).then_inc(again_in, 16)
                    sp.dma_start(gru_bias[:, 0:3 * FD], a["bih"]).then_inc(again_in, 16)
                    sp.dma_start(gb[:], a["bhh"]).then_inc(again_in, 16)
                    sp.dma_start(x[:], a["x_nodes"]).then_inc(again_in, 16)
                    sp.wait_ge(again_in, 64)

                @block.vector
                def _(dve):
                    dve.wait_ge(again_in, 64)
                    nc.vector.tensor_tensor(gru_bias[:, 0:2 * FD], gru_bias[:, 0:2 * FD], gb[:, 0:2 * FD],
                                            ALU.add).then_inc(gb_done, 1)
                    nc.vector.tensor_copy(gru_bias[:, 3 * FD:], gb[:, 2 * FD:]).then_inc(gb_done, 1)
                    dve.wait_ge(gb_done, 2)
            dense("l0", FD, None, "gru", None, None, dis1, tables[0], xT=xT2)

        with ExitStack() as c:
            rec_rows = sb("rec_rows", [P, GTR // P, P, 2], F32, c)
            ps_g = c.enter_context(nc.psum_tensor("ps_g", [P, 2, 1024], F32))
            rec_in, rec_turned, rec_read = sem("rec_in"), sem("rec_turned"), sem("rec_read")
            with nc.Block() as block:
                @block.sync
                def _(sp):
                    sp.dma_start(rec_rows[:].rearrange("p b e w -> p b (e w)"),
                                 groups.rearrange("(b p e) w -> p b (e w)", p=P, e=P)).then_inc(rec_in, 16)

                @block.tensor
                def _(pe):
                    pe.wait_ge(rec_in, 16)
                    for q in range(2):
                        for b in range(GTR // P):
                            mm = nc.tensor.transpose(ps_g[:, q, b * P:(b + 1) * P], rec_rows[:, b, :, q], ident[:])
                        mm.then_inc(rec_turned, 1)

                @block.vector
                def _(dve):
                    dve.wait_ge(rec_turned, 1)
                    nc.vector.tensor_copy(g_local[:], ps_g[:, 0, 0:GTR]).then_inc(rec_read, 1)
                    dve.wait_ge(rec_turned, 2)
                    nc.vector.tensor_copy(g_src_i[:], ps_g[:, 1, 0:GTR]).then_inc(rec_read, 1)
                    dve.wait_ge(rec_read, 2)

        sparse_pass("l1f", tables[0], FD, src_i, local, first_i, STEPS, W)
        sparse_pass("l1r", tables[0], FD, g_src_i, g_local, g_first_i, GSTEPS, P, rounds=False)
        dense("l1", FD, [(l1w[:], 0)], "relu", dis1, l1b, dis2, tables[1])
        clear_sems()
        sparse_pass("l2", tables[1], FD, src_i, local, first_i, STEPS, W)
        dense("l2", FD, [(l2w[:], 0)], "prelu", dis2, l2b, dis3, tables[2])
        sparse_pass("l3a", tables[2], FD, src_i, local, first_i, STEPS, W, weights=weight)
        dense("l3a", HID, [(l3w1[:], 0)], "hidden", dis3, l3b1, dis3, h_tables[0])
        sparse_pass("l3b", h_tables[0], HID, src_i, local, first_i, STEPS, W, weights=weight)
        dense("l3b", HID, [(l3w2[:, k, :], k) for k in range(2)], "hidden", dis3, l3b2, dis3, h_tables[1])
        sparse_pass("l3c", h_tables[1], HID, src_i, local, first_i, STEPS, W, weights=weight)
        dense("l3c", FD, [(l3w3[:, k, :], k) for k in range(2)], "linear", dis3, l3b3, None, None, last=True)


def kernel(**inputs):
    import numpy as np
    import concourse.bacc as bacc
    from concourse.bass_utils import run_bass_kernel_spmd

    i = {k: np.asarray(v) for k, v in inputs.items()}

    def padded(v, n, fill):
        return np.concatenate([v, np.full((n - v.shape[0],) + v.shape[1:], fill, v.dtype)])

    def cols(v, fill):
        return padded(v, T * P, fill).reshape(T, P).T

    def rep(v, n=P):
        return np.broadcast_to(v[None, :], (n, v.shape[0]))

    x = padded(i["x"], NP, 0)
    w1 = i["L0_gnn_W1"]
    f = np.float32
    arrays = {
        "dst_rows": padded(i["dst"].astype(np.int32), TR * P, PAD_NODE).reshape(TR // P, P, P).transpose(1, 0, 2),
        "src_cols": cols(i["src"].astype(np.int32), PAD_NODE),
        "dst_cols": cols(i["dst"].astype(np.int32), PAD_NODE),
        "w_cols": cols(i["edge_weight"], 0),
        "edge_feat": np.concatenate([padded(i["edge_attr_64"], T * P, 0).T, np.ones((1, T * P), f)]),
        "x_nodes": x.reshape(NB, P, FD).transpose(1, 0, 2),
        "x_feat": x.T,
        "wihT": i["L0_gnn_Wih"].T,
        "whhT": i["L0_gnn_Whh"].T,
        "w2": i["L0_gnn_W2"],
        "b2r": np.broadcast_to(i["L0_gnn_b2"][:, None], (P, P)),
        "w1xT": w1[:, :FD].T,
        "w1eT": np.concatenate([w1[:, FD:].T, i["L0_gnn_b1"][None, :]]),
        "bih": i["L0_gnn_bih"][None, :],
        "bhh": i["L0_gnn_bhh"][None, :],
        "l1w": i["L1_gnn_W"].T,
        "l2w": i["L2_gnn_W"],
        "l3w1": i["L3_gnn_W1"],
        "l3w2": i["L3_gnn_W2"].reshape(2, P, HID).transpose(1, 0, 2),
        "l3w3": i["L3_gnn_W3"].reshape(2, P, FD).transpose(1, 0, 2),
        "biases": np.concatenate([rep(i[k]) for k in ("L1_gnn_bias", "L2_gnn_b", "L3_gnn_b3", "L3_gnn_b1",
                                                      "L3_gnn_b2", "L2_gnn_prelu_w")], axis=1),
    }
    nc = bacc.Bacc("TRN2", target_bir_lowering=False, num_devices=1)
    given, aps = {}, {}
    for name, v in arrays.items():
        v = np.ascontiguousarray(v)
        given[f"in_{name}"] = v
        aps[name] = nc.dram_tensor(f"in_{name}", v.shape, mybir.dt.from_np(v.dtype), kind="ExternalInput").ap()
    out = nc.dram_tensor("out", (N, FD), F32, kind="ExternalOutput").ap()
    build(nc, aps, out)
    r = run_bass_kernel_spmd(nc, [given], core_ids=[0])
    return r.results[0]["out"]
```

```python
from contextlib import ExitStack

import concourse.bass as bass
from concourse import mybir

P = 128
N = 6250
E = 106250
FD = 128
ED = 64
HID = 256
NB = (N + P - 1) // P
NP = NB * P
TS = 16
PT = TS // 2
STEPS = -(-E // (P * TS))
T = STEPS * TS
TR = -(-T // P) * P
GSTEPS = -(-((T * P + NB * (P - 1)) // P) // TS)
GT = GSTEPS * TS
GTR = -(-GT // P) * P
W = 32
PAD_NODE = N
HOLE = 255.0
CB = 7
CHUNKS = NB // CB
EPS = 1e-5
assert CHUNKS * CB == NB and E <= T * P

F32 = mybir.dt.float32
BF16 = mybir.dt.bfloat16
I32 = mybir.dt.int32
U32 = mybir.dt.uint32
ALU = mybir.AluOpType
ACT = mybir.ActivationFunctionType
AX = mybir.AxisListType


def free_at_first(eng, *sems):
    for sem in sems:
        eng.sem_inc(sem, 1)


class Chain:

    def __init__(self, eng, sem):
        self.eng, self.sem, self.n = eng, sem, 0

    def step(self, ins):
        self.n += 1
        ins.then_inc(self.sem, 1)
        self.eng.wait_ge(self.sem, self.n)


def wait_apart(eng, sem, value, passed):
    eng.wait_ge(sem, value)
    eng.sem_inc(passed, 1)


def per_row(col, n):
    return col.unsqueeze(2).to_broadcast([col.shape[0], col.shape[1], n])


def per_block(row, k):
    return row.unsqueeze(1).to_broadcast([row.shape[0], k, row.shape[1]])


def build(nc, a, out):
    with ExitStack() as ctx:
        def sb(name, shape, dt=F32, c=ctx):
            return c.enter_context(nc.sbuf_tensor(name, shape, dt))

        phase_sems = []

        def sem(name):
            phase_sems.append(nc.alloc_semaphore(name=name))
            return phase_sems[-1]

        def clear_sems():
            nc.all_engine_barrier()
            nc.clear_and_free_semaphores(list(phase_sems))
            nc.all_engine_barrier()
            phase_sems.clear()

        p_table = nc.dram_tensor("p_table", [NP, FD], F32).ap()
        tables = [nc.dram_tensor(f"x_table{i}", [NP, FD], F32).ap() for i in range(3)]
        h_tables = [nc.dram_tensor(f"h_table{i}", [NP, HID], F32).ap() for i in range(2)]
        groups = nc.dram_tensor("groups", [GTR * P, 2], F32).ap()

        iota_row = sb("iota_row", [P, P])
        ident = sb("ident", [P, P])
        ones = sb("ones", [P, P])
        src_i = sb("src_i", [P, T], I32)
        dst_i = sb("dst_i", [P, T], I32)
        weight = sb("weight", [P, T])
        local0 = sb("local0", [P, T])
        local = sb("local", [P, T])
        first = sb("first", [1, TR])
        first0 = sb("first0", [1, TR])
        first_i = sb("first_i", [1, TR], I32)
        rounds_i = sb("rounds_i", [P, 1], I32)
        g_local = sb("g_local", [P, GTR])
        g_src_i = sb("g_src_i", [P, GTR], I32)
        g_first_i = sb("g_first_i", [1, GTR], I32)
        dis1 = sb("dis1", [P, NB])
        dis2 = sb("dis2", [P, NB])
        dis3 = sb("dis3", [P, NB])
        indeg = sb("indeg", [P, NB])
        wihT = sb("wihT", [P, 3 * FD])
        whhT = sb("whhT", [P, 3 * FD])
        w2 = sb("w2", [P, FD])
        b2r = sb("b2r", [P, P])
        w1xT = sb("w1xT", [P, FD])
        w1eT = sb("w1eT", [ED + 1, FD])
        l1w = sb("l1w", [P, FD])
        l2w = sb("l2w", [P, FD])
        l3w1 = sb("l3w1", [P, HID])
        l3w2 = sb("l3w2", [P, 2, HID])
        l3w3 = sb("l3w3", [P, 2, FD])
        biases = sb("biases", [P, 3 * FD + 2 * HID + 1])
        l1b, l2b, l3b3 = (biases[:, i * FD:(i + 1) * FD] for i in range(3))
        l3b1, l3b2 = (biases[:, 3 * FD + i * HID:3 * FD + (i + 1) * HID] for i in range(2))
        prelu = biases[:, 3 * FD + 2 * HID:3 * FD + 2 * HID + 1]
        gru_bias = sb("gru_bias", [1, 4 * FD])
        wcT = sb("wcT", [P, 3 * FD])
        bv = sb("bv", [P, 4 * FD])


        with ExitStack() as c:
            iota_i = sb("iota_i", [P, P], I32, c)
            row_i = sb("row_i", [P, 1], I32, c)
            row_f = sb("row_f", [P, 1], F32, c)
            rows_i = sb("rows_i", [P, TR // P, P], I32, c)
            rows_f = sb("rows_f", [P, TR // P, P], F32, c)
            lo = sb("lo", [P, TR // P], F32, c)
            hi = sb("hi", [P, TR // P], F32, c)
            diag = sb("diag", [P, 2, TR // P, P], F32, c)
            rep = sb("rep", [P, 2, TR], F32, c)
            span = sb("span", [P, T], F32, c)
            span_i = sb("span_i", [P, T], I32, c)
            span_m = sb("span_m", [P, 1], F32, c)
            ps_rep = c.enter_context(nc.psum_tensor("ps_rep", [P, 2, 1024], F32))
            ps_w = c.enter_context(nc.psum_tensor("ps_w", [P, 2, 512], F32))
            edges_in, rows_in, weights_in, iotas = sem("edges_in"), sem("rows_in"), sem("weights_in"), sem("iotas")
            a_dve, diags_done, rep_done, wmul_done = sem("a_dve"), sem("diags_done"), sem("rep_done"), sem("wmul_done")
            ones_done = sem("ones_done")
            with nc.Block() as block:
                @block.sync
                def _(sp):
                    sp.dma_start(rows_i[:], a["dst_rows"]).then_inc(rows_in, 16)
                    sp.dma_start(src_i[:], a["src_cols"]).then_inc(edges_in, 16)
                    sp.dma_start(dst_i[:], a["dst_cols"]).then_inc(edges_in, 16)
                    sp.dma_start(weight[:], a["w_cols"]).then_inc(edges_in, 16)
                    loads = [(wihT, "wihT"), (whhT, "whhT"), (w2, "w2"), (b2r, "b2r"), (w1xT, "w1xT"), (w1eT, "w1eT"),
                             (l1w, "l1w"), (l2w, "l2w"), (l3w1, "l3w1"), (l3w2, "l3w2"), (l3w3, "l3w3"),
                             (biases, "biases")]
                    for to, name in loads:
                        sp.dma_start(to[:], a[name]).then_inc(weights_in, 16)
                    sp.wait_ge(edges_in, 48)
                    sp.wait_ge(weights_in, 16 * len(loads))

                @block.gpsimd
                def _(pool):
                    nc.gpsimd.iota(iota_i[:], [[1, P]], base=0, channel_multiplier=0).then_inc(iotas, 1)
                    nc.gpsimd.iota(row_i[:], [[1, 1]], base=0, channel_multiplier=1).then_inc(iotas, 1)

                @block.vector
                def _(dve):
                    chain = Chain(dve, a_dve)
                    nc.vector.memset(ones[:], 1.0).then_inc(ones_done, 1)
                    dve.wait_ge(iotas, 2)
                    chain.step(nc.vector.tensor_copy(iota_row[:], iota_i[:]))
                    chain.step(nc.vector.tensor_copy(row_f[:], row_i[:]))
                    chain.step(nc.vector.tensor_scalar(ident[:], iota_row[:], row_f[:, 0:1], None, ALU.is_equal))
                    dve.wait_ge(rows_in, 16)
                    chain.step(nc.vector.tensor_copy(rows_f[:], rows_i[:]))
                    chain.step(nc.vector.tensor_reduce(lo[:], rows_f[:], AX.X, ALU.min))
                    chain.step(nc.vector.tensor_reduce(hi[:], rows_f[:], AX.X, ALU.max))
                    for q, v in enumerate((lo, hi)):
                        nc.vector.tensor_tensor(diag[:, q], per_block(ident[:], TR // P), per_row(v[:], P),
                                                ALU.mult).then_inc(diags_done, 1)
                    dve.wait_ge(rep_done, 1)
                    chain.step(nc.vector.tensor_copy(rep[:], ps_rep[:, :, 0:TR]))
                    dve.wait_ge(edges_in, 48)
                    chain.step(nc.vector.tensor_copy(span[:], dst_i[:]))
                    chain.step(nc.vector.tensor_tensor(local0[:], span[:], rep[:, 0, 0:T], ALU.subtract))
                    chain.step(nc.vector.tensor_copy(first0[:], rep[0:1, 0, :]))
                    chain.step(nc.vector.tensor_tensor(span[:], rep[:, 1, 0:T], rep[:, 0, 0:T], ALU.subtract))
                    chain.step(nc.vector.tensor_reduce(span_m[:], span[:], AX.X, ALU.max))
                    chain.step(nc.vector.tensor_copy(span_i[:, 0:1], span_m[:]))
                    chain.step(nc.vector.tensor_scalar(span_i[:, 1:2], span_i[:, 0:1], W.bit_length() - 1, None,
                                                       ALU.arith_shift_right))
                    chain.step(nc.vector.tensor_copy(span_m[:], span_i[:, 1:2]))
                    chain.step(nc.vector.tensor_scalar(span_m[:], span_m[:], 1.0, None, ALU.add))
                    chain.step(nc.vector.tensor_copy(rounds_i[:], span_m[:]))
                    dve.wait_ge(wmul_done, 1)
                    chain.step(nc.vector.tensor_copy(wcT[:], ps_w[:, 0, 0:3 * FD]))
                    chain.step(nc.vector.tensor_copy(bv[:, 0:3 * FD], ps_w[:, 1, 0:3 * FD]))
                    chain.step(nc.vector.memset(bv[:, 3 * FD:], 0.0))

                @block.tensor
                def _(pe):
                    pe.wait_ge(ones_done, 1)
                    pe.wait_ge(diags_done, 2)
                    for q in range(2):
                        for b in range(TR // P):
                            mm = nc.tensor.matmul(ps_rep[:, q, b * P:(b + 1) * P], ones[:], diag[:, q, b, :],
                                                  start=True, stop=True)
                    mm.then_inc(rep_done, 1)
                    pe.wait_ge(weights_in, 16 * 12)
                    nc.tensor.matmul(ps_w[:, 0, 0:3 * FD], w2[:], wihT[:], start=True, stop=True)
                    nc.tensor.matmul(ps_w[:, 1, 0:3 * FD], b2r[:], wihT[:], start=True, stop=True).then_inc(wmul_done, 1)

        with ExitStack() as c:
            src_blk = sb("src_blk", [P, T], F32, c)
            src_row = sb("src_row", [P, T], F32, c)
            dst_blk = sb("dst_blk", [P, T], F32, c)
            dst_row = sb("dst_row", [P, T], F32, c)
            place = sb("place", [P, T], F32, c)
            record = sb("record", [P, T, 2], F32, c)
            xT = sb("xT", [P, NP], F32, c)
            before_i = sb("before_i", [P, T], I32, c)
            tri_b = sb("tri_b", [P, P], BF16, c)
            in_blk = sb("in_blk", [P, 2, TS, NB], BF16, c)
            pre = sb("pre", [NB, T], F32, c)
            with ExitStack() as c2:
                tri = sb("tri", [P, P], F32, c2)
                ones_b = sb("ones_b", [P, 1], BF16, c2)
                holes = sb("holes", [P, GTR, 2], F32, c2)
                count = sb("count", [NB, T], F32, c2)
                upto = sb("upto", [NB, T], F32, c2)
                ones_t = sb("ones_t", [NB, T], F32, c2)
                size = sb("size", [NB, 4], F32, c2)
                size_i = sb("size_i", [NB, 3], I32, c2)
                col = sb("col", [P, 1], F32, c2)
                col_i = sb("col_i", [P, 1], I32, c2)
                tile_i = sb("tile_i", [NB, GTR], I32, c2)
                tile_f = sb("tile_f", [NB, GTR], F32, c2)
                ended = sb("ended", [NB, GTR], F32, c2)
                g_first = sb("g_first", [1, GTR], F32, c2)
                ps_cnt = c2.enter_context(nc.psum_tensor("ps_cnt", [P, 2, 512], F32))
                ps_map = c2.enter_context(nc.psum_tensor("ps_map", [P, 2, 512], F32))
                ps_base = c2.enter_context(nc.psum_tensor("ps_base", [P, 512], F32))
                b_dve, holes_out, holes_set, b_iota = sem("b_dve"), sem("holes_out"), sem("holes_set"), sem("b_iota")
                xt_in = sem("xt_in")
                blk_ready = [sem(f"blk_ready{h}") for h in range(2)]
                blk_counted = [sem(f"blk_counted{h}") for h in range(2)]
                counts_read = [sem(f"counts_read{h}") for h in range(2)]
                
                size_ready, base_done, ended_ready, map_done = sem("size_ready"), sem("base_done"), sem("ended_ready"), sem("map_done")
                PSTEPS = T // TS
                with nc.Block() as block:
                    @block.sync
                    def _(sp):
                        sp.dma_start(xT[:], a["x_feat"]).then_inc(xt_in, 16)
                        sp.wait_ge(holes_set, 2)
                        sp.dma_start(groups.rearrange("(p t) w -> p (t w)", p=P),
                                     holes[:].rearrange("p t w -> p (t w)")).then_inc(holes_out, 16)
                        sp.wait_ge(holes_out, 16)
                        sp.wait_ge(xt_in, 16)

                    @block.gpsimd
                    def _(pool):
                        nc.gpsimd.memset(holes[:, :, 0], HOLE).then_inc(holes_set, 1)
                        nc.gpsimd.memset(holes[:, :, 1], 0.0).then_inc(holes_set, 1)
                        nc.gpsimd.iota(tile_i[:], [[P, GTR]], base=0, channel_multiplier=0).then_inc(b_iota, 1)
                        nc.gpsimd.iota(col_i[:], [[1, 1]], base=0, channel_multiplier=1).then_inc(b_iota, 1)

                    @block.vector
                    def _(dve):
                        chain = Chain(dve, b_dve)
                        for idx, blk, row in ((src_i, src_blk, src_row), (dst_i, dst_blk, dst_row)):
                            chain.step(nc.vector.tensor_scalar(before_i[:], idx[:], 7, None, ALU.arith_shift_right))
                            chain.step(nc.vector.tensor_copy(blk[:], before_i[:]))
                            chain.step(nc.vector.tensor_scalar(before_i[:], idx[:], P - 1, None, ALU.bitwise_and))
                            chain.step(nc.vector.tensor_copy(row[:], before_i[:]))
                        chain.step(nc.vector.tensor_copy(record[:, :, 0], src_row[:]))
                        chain.step(nc.vector.tensor_copy(record[:, :, 1], dst_i[:]))
                        dve.wait_ge(b_iota, 2)
                        chain.step(nc.vector.tensor_copy(col[:], col_i[:]))
                        chain.step(nc.vector.tensor_copy(tile_f[:], tile_i[:]))
                        chain.step(nc.vector.tensor_scalar(tri[:], iota_row[:], col[:, 0:1], None, ALU.is_gt))
                        chain.step(nc.vector.tensor_copy(tri_b[:], tri[:]))
                        chain.step(nc.vector.memset(ones_b[:], 1.0))
                        chain.step(nc.vector.memset(ones_t[:], 1.0))
                        free_at_first(dve, *counts_read)
                        with dve.Fori(0, PSTEPS // 2) as i:
                            for h in range(2):
                                t0 = i * (2 * TS) + h * TS
                                nc.vector.tensor_tensor(in_blk[:, h], per_block(iota_row[:, 0:NB], TS),
                                                        per_row(src_blk[:, bass.ds(t0, TS)], NB),
                                                        ALU.is_equal).then_inc(blk_ready[h], 1)
                            for h in range(2):
                                t0 = i * (2 * TS) + h * TS
                                dve.wait_ge(blk_counted[h], i + 1)
                                nc.vector.tensor_copy(count[:, bass.ds(t0, TS)],
                                                      ps_cnt[0:NB, h, 0:TS]).then_inc(counts_read[h], 1)
                        for h in range(2):
                            dve.wait_ge(counts_read[h], PSTEPS // 2 + 1)
                        chain.step(nc.vector.tensor_tensor_scan(upto[:], ones_t[:], count[:], 0.0, ALU.mult, ALU.add))
                        chain.step(nc.vector.tensor_scalar(size[:, 0:1], upto[:, T - 1:T], float(P - 1), None, ALU.add))
                        chain.step(nc.vector.tensor_copy(size_i[:, 0:1], size[:, 0:1]))
                        chain.step(nc.vector.tensor_scalar(size_i[:, 1:2], size_i[:, 0:1], -P, None, ALU.bitwise_and))
                        nc.vector.tensor_copy(size[:, 1:2], size_i[:, 1:2]).then_inc(size_ready, 1)
                        dve.wait_ge(size_ready, 1)
                        dve.wait_ge(base_done, 1)
                        chain.step(nc.vector.tensor_copy(size[:, 2:3], ps_base[0:NB, 0:1]))
                        chain.step(nc.vector.tensor_tensor(size[:, 3:4], size[:, 2:3], size[:, 1:2], ALU.add))
                        nc.vector.tensor_scalar(ended[:], tile_f[:], size[:, 3:4], None,
                                                ALU.is_ge).then_inc(ended_ready, 1)
                        chain.step(nc.vector.tensor_tensor(pre[:], upto[:], count[:], ALU.subtract))
                        chain.step(nc.vector.tensor_scalar(pre[:], pre[:], size[:, 2:3], None, ALU.add))
                        dve.wait_ge(map_done, 1)
                        for q in range(2):
                            chain.step(nc.vector.tensor_scalar(g_first[:, q * (GTR // 2):(q + 1) * (GTR // 2)],
                                                               ps_map[0:1, q, 0:GTR // 2], float(NB - 1), float(P),
                                                               ALU.min, ALU.mult))
                        chain.step(nc.vector.tensor_copy(g_first_i[:], g_first[:]))

                    @block.tensor
                    def _(pe):
                        with pe.Fori(0, PSTEPS // 2) as i:
                            for h in range(2):
                                pe.wait_ge(blk_ready[h], i + 1)
                                pe.wait_ge(counts_read[h], i + 1)
                                for t in range(TS):
                                    mm = nc.tensor.matmul(ps_cnt[0:NB, h, t:t + 1], in_blk[:, h, t, :], ones_b[:],
                                                          start=True, stop=True)
                                mm.then_inc(blk_counted[h], 1)
                        pe.wait_ge(size_ready, 1)
                        nc.tensor.matmul(ps_base[0:NB, 0:1], tri[0:NB, 0:NB], size[:, 1:2], start=True,
                                         stop=True).then_inc(base_done, 1)
                        pe.wait_ge(ended_ready, 1)
                        for q in range(2):
                            mm = nc.tensor.matmul(ps_map[:, q, 0:GTR // 2], ones[0:NB, :],
                                                  ended[:, q * (GTR // 2):(q + 1) * (GTR // 2)], start=True, stop=True)
                        mm.then_inc(map_done, 1)

            with ExitStack() as c2:
                idx_buf = sb("idx_buf", [P, 2, PT], I32, c2)
                rec_buf = sb("rec_buf", [P, 2, PT, 2], F32, c2)
                deg_src = sb("deg_src", [P, 2, PT, P], BF16, c2)
                deg_dst = sb("deg_dst", [P, 2, PT, 2, P], F32, c2)
                blk_src = sb("blk_src", [P, 2, PT, NB], BF16, c2)
                blk_dst = sb("blk_dst", [P, 2, PT, NB], F32, c2)
                deg_t = sb("deg_t", [NB, 3, P], F32, c2)
                deg = sb("deg", [P, 4, NB], F32, c2)
                zero = sb("zero", [P, 2 * P], F32, c2)
                p_sb = sb("p_sb", [P, NB, FD], F32, c2)
                ps_src = c2.enter_context(nc.psum_tensor("ps_src", [P, 512], F32))
                ps_dst = c2.enter_context(nc.psum_tensor("ps_dst", [P, 512], F32))
                ps_deg = c2.enter_context(nc.psum_tensor("ps_deg", [P, 512], F32))
                ps_p = c2.enter_context(nc.psum_tensor("ps_p", [P, 2, 512], F32))
                spread = sb("spread", [NB, 2, PT, NB], F32, c2)
                picked = sb("picked", [P, 2, PT, NB], F32, c2)
                ps_pos = c2.enter_context(nc.psum_tensor("ps_pos", [P, 2, 512], F32))
                place_ready = [sem(f"place_ready{h}") for h in range(2)]
                place_mul = [sem(f"place_mul{h}") for h in range(2)]
                place_read = [sem(f"place_read{h}") for h in range(2)]
                pick_done = sem("pick_done")
                put = [sem(f"put{h}") for h in range(2)]
                put_ready = [sem(f"put_ready{h}") for h in range(2)]
                c_dve, c_pe, deg_eq = sem("c_dve"), sem("c_pe"), sem("deg_eq")
                hots_ready = [sem(f"hots_ready{h}") for h in range(2)]
                hots_used = [sem(f"hots_used{h}") for h in range(2)]
                deg_done, degt_ready, degT_done = sem("deg_done"), sem("degt_ready"), sem("degT_done")
                zero_set, deg_cleared = sem("zero_set"), sem("deg_cleared")
                p_mul, p_read, p_out, root_in, root_out = sem("p_mul"), sem("p_read"), sem("p_out"), sem("root_in"), sem("root_out")
                passed = sem("passed_put")
                PG = [(j, min(4, NB - j)) for j in range(0, NB, 4)]
                with nc.Block() as block:
                    @block.gpsimd
                    def _(pool):
                        with pool.Fori(0, STEPS) as i:
                            for h in range(2):
                                wait_apart(pool, put_ready[h], i * 2 + 2, passed)
                                for t in range(PT):
                                    pool.indirect_dma_start(
                                        groups, bass.IndirectOffsetOnAxis(idx_buf[:, h, t:t + 1].bitcast(U32), 0),
                                        rec_buf[:, h, t, :], None).then_inc(put[h], 16)
                        for h in range(2):
                            pool.wait_ge(put[h], 16 * PT * STEPS)

                    @block.scalar
                    def _(act):
                        def fill(i, h):
                            t0 = i * TS + h * PT
                            act.wait_ge(place_read[h], i + 2)
                            nc.scalar.copy(idx_buf[:, h, :], place[:, bass.ds(t0, PT)]).then_inc(put_ready[h], 1)
                            nc.scalar.copy(rec_buf[:, h], record[:, bass.ds(t0, PT), :]).then_inc(put_ready[h], 1)

                        for h in range(2):
                            fill(0, h)
                        with act.Fori(1, STEPS) as i:
                            for h in range(2):
                                act.wait_ge(put[h], i * (16 * PT))
                                fill(i, h)
                        act.wait_ge(root_in, 1)
                        nc.scalar.activation(deg[:, 0:3, :], deg[:, 0:3, :], ACT.Sqrt).then_inc(root_out, 1)

                    @block.sync
                    def _(sp):
                        sp.wait_ge(p_read, len(PG))
                        sp.dma_start(p_table.rearrange("(b p) f -> p b f", p=P), p_sb[:]).then_inc(p_out, 16)
                        sp.wait_ge(p_out, 16)

                    @block.vector
                    def _(dve):
                        chain = Chain(dve, c_dve)
                        free_at_first(dve, *place_read)
                        nc.vector.memset(zero[:], 0.0).then_inc(zero_set, 1)
                        dve.wait_ge(zero_set, 1)
                        with dve.Fori(0, STEPS) as i:
                            for h in range(2):
                                t0 = i * TS + h * PT
                                nc.vector.tensor_tensor(in_blk[:, h, 0:PT], per_block(iota_row[:, 0:NB], PT),
                                                        per_row(src_blk[:, bass.ds(t0, PT)], NB),
                                                        ALU.is_equal).then_inc(place_ready[h], 1)
                                nc.vector.tensor_tensor(spread[:, h], per_block(ident[0:NB, 0:NB], PT),
                                                        per_row(pre[:, bass.ds(t0, PT)], NB),
                                                        ALU.mult).then_inc(place_ready[h], 1)
                            for h in range(2):
                                t0 = i * TS + h * PT
                                dve.wait_ge(place_mul[h], i + 1)
                                nc.vector.tensor_tensor(picked[:, h], in_blk[:, h, 0:PT],
                                                        ps_pos[:, h, 0:PT * NB].rearrange("p (t b) -> p t b", b=NB),
                                                        ALU.mult).then_inc(pick_done, 1)
                                dve.wait_ge(pick_done, i * 2 + (h + 1))
                                nc.vector.tensor_reduce(place[:, bass.ds(t0, PT)], picked[:, h], AX.X,
                                                        ALU.add).then_inc(place_read[h], 1)
                            for h in range(2):
                                t0 = i * TS + h * PT
                                dve.wait_ge(hots_used[h], i + 1)
                                nc.vector.tensor_tensor(deg_src[:, h], per_block(iota_row[:], PT),
                                                        per_row(src_row[:, bass.ds(t0, PT)], P),
                                                        ALU.is_equal).then_inc(hots_ready[h], 1)
                                nc.vector.tensor_tensor(blk_src[:, h], per_block(iota_row[:, 0:NB], PT),
                                                        per_row(src_blk[:, bass.ds(t0, PT)], NB),
                                                        ALU.is_equal).then_inc(hots_ready[h], 1)
                                nc.vector.tensor_tensor(blk_dst[:, h], per_block(iota_row[:, 0:NB], PT),
                                                        per_row(dst_blk[:, bass.ds(t0, PT)], NB),
                                                        ALU.is_equal).then_inc(hots_ready[h], 1)
                                nc.vector.tensor_tensor(deg_dst[:, h, :, 0, :], per_block(iota_row[:], PT),
                                                        per_row(dst_row[:, bass.ds(t0, PT)], P),
                                                        ALU.is_equal).then_inc(deg_eq, 1)
                                dve.wait_ge(deg_eq, i * 2 + (h + 1))
                                nc.vector.tensor_tensor(deg_dst[:, h, :, 1, :], deg_dst[:, h, :, 0, :],
                                                        per_row(weight[:, bass.ds(t0, PT)], P),
                                                        ALU.mult).then_inc(hots_ready[h], 1)
                        for q, (j, n) in enumerate(PG):
                            dve.wait_ge(p_mul, q + 1)
                            nc.vector.tensor_copy(p_sb[:, j:j + n, :], ps_p[:, q % 2, 0:n * FD].rearrange(
                                "p (b f) -> p b f", f=FD)).then_inc(p_read, 1)
                        dve.wait_ge(deg_done, 1)
                        nc.vector.tensor_copy(deg_t[:, 0, :], ps_src[0:NB, 0:P]).then_inc(degt_ready, 1)
                        nc.vector.tensor_copy(deg_t[:, 1:3, :], ps_dst[0:NB, 0:2 * P].rearrange(
                            "b (q r) -> b q r", r=P)).then_inc(degt_ready, 1)
                        dve.wait_ge(degT_done, 1)
                        chain.step(nc.vector.tensor_copy(indeg[:], ps_deg[:, NB:2 * NB]))
                        chain.step(nc.vector.tensor_scalar(deg[:, 1, :], indeg[:], 1.0, None, ALU.add))
                        chain.step(nc.vector.tensor_tensor(deg[:, 0, :], deg[:, 1, :], ps_deg[:, 0:NB], ALU.add))
                        chain.step(nc.vector.tensor_scalar(deg[:, 2, :], ps_deg[:, 2 * NB:3 * NB], 1.0, None, ALU.add))
                        chain.step(nc.vector.tensor_scalar(deg[:, 3, :], deg[:, 2, :], 0.0, None, ALU.is_gt))
                        chain.step(nc.vector.tensor_scalar(deg[:, 0:2, :], deg[:, 0:2, :], 1.0, None, ALU.max))
                        nc.vector.tensor_scalar(deg[:, 2, :], deg[:, 2, :], 1e-30, None, ALU.max).then_inc(root_in, 1)
                        dve.wait_ge(root_out, 1)
                        chain.step(nc.vector.reciprocal(dis1[:], deg[:, 0, :]))
                        chain.step(nc.vector.reciprocal(dis2[:], deg[:, 1, :]))
                        chain.step(nc.vector.reciprocal(dis3[:], deg[:, 2, :]))
                        chain.step(nc.vector.tensor_tensor(dis3[:], dis3[:], deg[:, 3, :], ALU.mult))

                    @block.tensor
                    def _(pe):
                        free_at_first(pe, *hots_used)
                        pe.wait_ge(zero_set, 1)
                        nc.tensor.matmul(ps_src[0:NB, 0:P], zero[:, 0:NB], zero[:, 0:P], start=True, stop=False)
                        nc.tensor.matmul(ps_dst[0:NB, 0:2 * P], zero[:, 0:NB], zero[:], start=True, stop=False)
                        with pe.Fori(0, STEPS) as i:
                            for h in range(2):
                                pe.wait_ge(place_ready[h], i * 2 + 2)
                                pe.wait_ge(place_read[h], i + 1)
                                nc.tensor.matmul(ps_pos[:, h, 0:PT * NB], tri_b[:],
                                                 in_blk[:, h, 0:PT].rearrange("p t b -> p (t b)"), start=True, stop=False)
                                nc.tensor.matmul(ps_pos[:, h, 0:PT * NB], ones[0:NB, :],
                                                 spread[:, h].rearrange("p t b -> p (t b)"), start=False,
                                                 stop=True).then_inc(place_mul[h], 1)
                            for h in range(2):
                                pe.wait_ge(hots_ready[h], i * 4 + 4)
                                for t in range(PT):
                                    nc.tensor.matmul(ps_src[0:NB, 0:P], blk_src[:, h, t, :], deg_src[:, h, t, :],
                                                     start=False, stop=False)
                                    mm = nc.tensor.matmul(ps_dst[0:NB, 0:2 * P], blk_dst[:, h, t, :],
                                                          deg_dst[:, h, t].rearrange("p q r -> p (q r)"),
                                                          start=False, stop=False)
                                mm.then_inc(hots_used[h], 1)
                        nc.tensor.matmul(ps_src[0:NB, 0:P], zero[:, 0:NB], zero[:, 0:P], start=False, stop=True)
                        nc.tensor.matmul(ps_dst[0:NB, 0:2 * P], zero[:, 0:NB], zero[:], start=False, stop=True).then_inc(deg_done, 1)
                        for q, (j, n) in enumerate(PG):
                            if q >= 2:
                                pe.wait_ge(p_read, q - 1)
                            for b in range(n):
                                mm = nc.tensor.matmul(ps_p[:, q % 2, b * FD:(b + 1) * FD],
                                                      xT[:, (j + b) * P:(j + b + 1) * P], w1xT[:], start=True, stop=True)
                            mm.then_inc(p_mul, 1)
                        pe.wait_ge(degt_ready, 2)
                        for q in range(3):
                            mm = nc.tensor.transpose(ps_deg[:, q * NB:(q + 1) * NB], deg_t[:, q, :], ident[0:NB, 0:NB])
                        mm.then_inc(degT_done, 1)

        clear_sems()
        x = sb("x", [P, NB, FD])
        acc = sb("acc", [P, 2, NP + W])

        def sparse_pass(name, table, F, idx, local_src, first_src, tiles, TH, win, weights=None, rounds=True,
                        messages=None, loads=()):
            K = F // P
            steps = tiles // (2 * TH)
            with ExitStack() as c:
                ring = sb(f"ring_{name}", [P, 2, TH, F], F32, c)
                idx_buf = sb(f"idx_buf_{name}", [P, 2, TH], I32, c)
                hot = sb(f"hot_{name}", [P, 2, TH, win], F32, c)
                pa = c.enter_context(nc.psum_tensor(f"pa_{name}", [P, 2, max(512, TH * K * win)], F32))
                if messages:
                    edge = sb(f"edge_{name}", [ED + 1, 2, TH * P], F32, c)
                    msg = sb(f"msg_{name}", [P, 2, TH, FD], F32, c)
                    pm = c.enter_context(nc.psum_tensor(f"pm_{name}", [P, 2, TH * FD], F32))
                gathered = [sem(f"gathered_{name}{h}") for h in range(2)]
                idx_ready = [sem(f"idx_ready_{name}{h}") for h in range(2)]
                hot_ready = [sem(f"hot_ready_{name}{h}") for h in range(2)]
                summed = [sem(f"summed_{name}{h}") for h in range(2)]
                added = [sem(f"added_{name}{h}") for h in range(2)]
                add_chain, eq_done, round_set = sem(f"add_chain_{name}"), sem(f"eq_done_{name}"), sem(f"round_set_{name}")
                passed, passed_dve = sem(f"passed_{name}"), sem(f"passed_dve_{name}")
                if messages:
                    edge_in = [sem(f"edge_in_{name}{h}") for h in range(2)]
                    edge_mul = [sem(f"edge_mul_{name}{h}") for h in range(2)]
                    loaded = sem(f"loaded_{name}")
                    pre_done = [sem(f"pre_done_{name}{h}") for h in range(2)]
                    msg_done = [sem(f"msg_done_{name}{h}") for h in range(2)]

                def loops(eng, body):
                    if rounds:
                        n = eng.value_load(rounds_i[0:1, 0:1], min_val=1, max_val=NP // W)
                        with eng.Fori(0, n) as v:
                            body(v)
                    else:
                        body(0)

                with nc.Block() as block:
                    @block.gpsimd
                    def _(pool):
                        def a_round(v):
                            with pool.Fori(0, steps) as i:
                                done = v * steps + i
                                for h in range(2):
                                    wait_apart(pool, idx_ready[h], done + 1, passed)
                                    for t in range(TH):
                                        pool.indirect_dma_start(
                                            ring[:, h, t, :], None, table,
                                            bass.IndirectOffsetOnAxis(idx_buf[:, h, t:t + 1].bitcast(U32), 0)
                                        ).then_inc(gathered[h], 16)
                        loops(pool, a_round)

                    @block.scalar
                    def _(act):
                        def copy_idx(done, i, h):
                            act.wait_ge(summed[h], done + 1)
                            nc.scalar.copy(idx_buf[:, h, :], idx[:, bass.ds(i * (2 * TH) + h * TH, TH)]
                                           ).then_inc(idx_ready[h], 1)

                        def relu(done, h):
                            act.wait_ge(pre_done[h], done + 2)
                            nc.scalar.activation(msg[:, h], msg[:, h], ACT.Relu).then_inc(msg_done[h], 1)

                        def a_round(v):
                            if not messages:
                                with act.Fori(0, steps) as i:
                                    for h in range(2):
                                        copy_idx(v * steps + i, i, h)
                                return
                            for h in range(2):
                                copy_idx(v * steps, 0, h)
                            with act.Fori(0, steps - 1) as i:
                                for h in range(2):
                                    relu(v * steps + i, h)
                                    copy_idx(v * steps + i + 1, i + 1, h)
                            for h in range(2):
                                relu(v * steps + (steps - 1), h)
                        loops(act, a_round)

                    if messages:
                        @block.sync
                        def _(sp):
                            for to, what in loads:
                                sp.dma_start(to, what).then_inc(loaded, 16)

                            def a_round(v):
                                with sp.Fori(0, steps) as i:
                                    done = v * steps + i
                                    for h in range(2):
                                        sp.wait_ge(pre_done[h], done + 1)
                                        sp.dma_start(edge[:, h, :], messages[:, bass.ds((i * (2 * TH) + h * TH) * P, TH * P)]
                                                     ).then_inc(edge_in[h], 16)
                            loops(sp, a_round)
                            if loads:
                                sp.wait_ge(loaded, 16 * len(loads))

                    @block.tensor
                    def _(pe):
                        free_at_first(pe, *summed)

                        def edge_part(done, h):
                            pe.wait_ge(edge_in[h], done * 16 + 16)
                            pe.wait_ge(pre_done[h], done + 1)
                            for t in range(TH):
                                mm = nc.tensor.matmul(pm[:, h, t * FD:(t + 1) * FD], edge[:, h, t * P:(t + 1) * P],
                                                      w1eT[:], start=True, stop=True)
                            mm.then_inc(edge_mul[h], 1)

                        def sum_part(done, h):
                            if messages:
                                pe.wait_ge(msg_done[h], done + 1)
                            else:
                                pe.wait_ge(gathered[h], done * (16 * TH) + 16 * TH)
                            pe.wait_ge(hot_ready[h], done + 1)
                            pe.wait_ge(added[h], done + 1)
                            rows = msg if messages else ring
                            for t in range(TH):
                                for k in range(K):
                                    at = (t * K + k) * win
                                    mm = nc.tensor.matmul(pa[:, h, at:at + win], rows[:, h, t, k * P:(k + 1) * P],
                                                          hot[:, h, t, :], start=True, stop=True)
                            mm.then_inc(summed[h], 1)

                        def a_round(v):
                            if not messages:
                                with pe.Fori(0, steps) as i:
                                    for h in range(2):
                                        sum_part(v * steps + i, h)
                                return
                            edge_part(v * steps, 0)
                            with pe.Fori(0, steps - 1) as i:
                                edge_part(v * steps + i, 1)
                                sum_part(v * steps + i, 0)
                                edge_part(v * steps + i + 1, 0)
                                sum_part(v * steps + i, 1)
                            edge_part(v * steps + (steps - 1), 1)
                            for h in range(2):
                                sum_part(v * steps + (steps - 1), h)
                        loops(pe, a_round)

                    @block.vector
                    def _(dve):
                        free_at_first(dve, *added, *(pre_done if messages else []))
                        setup = 0
                        if rounds:
                            nc.vector.tensor_scalar(local[:], local0[:], float(W), None, ALU.add).then_inc(round_set, 1)
                            nc.vector.tensor_scalar(first[:], first0[:], float(-W), None, ALU.add).then_inc(round_set, 1)
                            setup = 2
                            if messages:
                                nc.vector.memset(acc[:], 0.0).then_inc(round_set, 1)
                                setup = 3

                        def a_round(v):
                            if rounds:
                                dve.wait_ge(round_set, v * 3 + setup)
                                nc.vector.tensor_scalar(local[:], local[:], float(-W), None, ALU.add
                                                        ).then_inc(round_set, 1)
                                nc.vector.tensor_scalar(first[:], first[:], float(W), float(NP), ALU.add, ALU.min
                                                        ).then_inc(round_set, 1)
                                dve.wait_ge(round_set, v * 3 + setup + 2)
                                nc.vector.tensor_copy(first_i[:], first[:]).then_inc(round_set, 1)
                                wait_apart(dve, round_set, v * 3 + setup + 3, passed_dve)
                            def one_hots(i, h):
                                done = v * steps + i
                                t0 = i * (2 * TH) + h * TH
                                eq = nc.vector.tensor_tensor(hot[:, h], per_block(iota_row[:, 0:win], TH),
                                                             per_row(local_src[:, bass.ds(t0, TH)], win), ALU.is_equal)
                                if weights is None:
                                    eq.then_inc(hot_ready[h], 1)
                                    return
                                eq.then_inc(eq_done, 1)
                                dve.wait_ge(eq_done, done * 2 + (h + 1))
                                nc.vector.tensor_tensor(hot[:, h], hot[:, h],
                                                        per_row(weights[:, bass.ds(t0, TH)], win),
                                                        ALU.mult).then_inc(hot_ready[h], 1)

                            def message_sum(i, h):
                                done = v * steps + i
                                dve.wait_ge(gathered[h], done * (16 * TH) + 16 * TH)
                                dve.wait_ge(edge_mul[h], done + 1)
                                nc.vector.tensor_tensor(msg[:, h].rearrange("p t f -> p (t f)"), pm[:, h],
                                                        ring[:, h].rearrange("p t f -> p (t f)"),
                                                        ALU.add).then_inc(pre_done[h], 1)

                            def add_sums(i, h):
                                done = v * steps + i
                                t0 = i * (2 * TH) + h * TH
                                ats = [dve.value_load(first_src[0:1, bass.ds(t0 + t, 1)], min_val=0,
                                                      max_val=NP + W - win) for t in range(TH)]
                                dve.wait_ge(summed[h], done + 2)
                                dve.wait_ge(added[1 - h], done + (2 if h else 1))
                                for t in range(TH):
                                    to = acc[:, 0:K, bass.ds(ats[t], win)]
                                    add = nc.vector.tensor_tensor(
                                        to, to, pa[:, h, t * K * win:(t + 1) * K * win].rearrange(
                                            "p (k n) -> p k n", k=K), ALU.add)
                                    if t < TH - 1:
                                        add.then_inc(add_chain, 1)
                                        dve.wait_ge(add_chain, done * (2 * (TH - 1)) + (h * (TH - 1) + t + 1))
                                    else:
                                        add.then_inc(added[h], 1)

                            if messages:
                                for h in range(2):
                                    one_hots(0, h)
                                    message_sum(0, h)
                                add_sums(0, 0)
                                with dve.Fori(1, steps) as i:
                                    one_hots(i, 0)
                                    message_sum(i, 0)
                                    add_sums(i - 1, 1)
                                    one_hots(i, 1)
                                    message_sum(i, 1)
                                    add_sums(i, 0)
                                add_sums(steps - 1, 1)
                            else:
                                with dve.Fori(0, steps) as i:
                                    for h in range(2):
                                        one_hots(i, h)
                                    for h in range(2):
                                        add_sums(i, h)
                        loops(dve, a_round)

        def dense(name, F, weights, kind, dis_in, bias, dis_out, table, last=False, xT=None):
            Kn = F // P
            with ExitStack() as c:
                width = 4 * FD if kind == "gru" else F
                y2 = sb(f"y_{name}", [P, 2, CB, F], F32, c)
                t1 = sb(f"t1_{name}", [P, CB, width], F32, c)
                small = sb(f"small_{name}", [P, 4, CB], F32, c)
                nbuf, cols_each = (6, 512) if kind == "gru" else (2, 1024) if F == FD else (1, CB * F)
                po = c.enter_context(nc.psum_tensor(f"po_{name}", [P, nbuf, cols_each], F32))
                pt = c.enter_context(nc.psum_tensor(f"pt_{name}", [P, 2, 512], F32))
                conv_done, conv_read, d_dve = sem(f"conv_done_{name}"), sem(f"conv_read_{name}"), sem(f"d_dve_{name}")
                act_in, act_out, rows_ready = sem(f"act_in_{name}"), sem(f"act_out_{name}"), sem(f"rows_ready_{name}")
                rows_out = [sem(f"rows_out_{name}{q}") for q in range(2)]
                turned, turned_read = sem(f"turned_{name}"), sem(f"turned_read_{name}")
                TP = [(k, q, min(4, CB - q)) for k in range(Kn) for q in range(0, CB, 4)]

                with nc.Block() as block:
                    @block.tensor
                    def _(pe):
                        def conv(ch):
                            for b in range(CB):
                                n = ch * CB + b
                                s = slice(n * P, (n + 1) * P)
                                if kind == "gru":
                                    if n >= nbuf:
                                        pe.wait_ge(conv_read, n - nbuf + 1)
                                    o = po[:, n % nbuf, :]
                                    for cols, terms in (
                                            (slice(0, 2 * FD), [(xT[:, s], whhT[:, 0:2 * FD]),
                                                                (acc[:, 0, s], wcT[:, 0:2 * FD])]),
                                            (slice(2 * FD, 3 * FD), [(acc[:, 0, s], wcT[:, 2 * FD:])]),
                                            (slice(3 * FD, 4 * FD), [(xT[:, s], whhT[:, 2 * FD:])])):
                                        nc.tensor.matmul(o[:, cols], ones[0:1, :], gru_bias[:, cols],
                                                         start=True, stop=False)
                                        for q, (node_part, w) in enumerate(terms):
                                            mm = nc.tensor.matmul(o[:, cols], node_part, w, start=False,
                                                                  stop=(q == len(terms) - 1))
                                    mm.then_inc(conv_done, 1)
                                else:
                                    if ch >= nbuf and b == 0:
                                        pe.wait_ge(conv_read, ch - nbuf + 1)
                                    for q, (w, k) in enumerate(weights):
                                        mm = nc.tensor.matmul(po[:, ch % nbuf, b * F:(b + 1) * F], acc[:, k, s], w,
                                                              start=(q == 0), stop=(q == len(weights) - 1))
                            if kind != "gru":
                                mm.then_inc(conv_done, 1)

                        def turn(ch):
                            pe.wait_ge(rows_ready, ch + 1)
                            for q, (k, b0, n) in enumerate(TP):
                                m = ch * len(TP) + q
                                if m >= 2:
                                    pe.wait_ge(turned_read, m - 1)
                                for b in range(n):
                                    mm = nc.tensor.transpose(pt[:, m % 2, b * P:(b + 1) * P],
                                                             y2[:, ch % 2, b0 + b, k * P:(k + 1) * P], ident[:])
                                mm.then_inc(turned, 1)

                        conv(0)
                        for ch in range(CHUNKS):
                            if ch < CHUNKS - 1:
                                conv(ch + 1)
                            if not last:
                                turn(ch)

                    @block.scalar
                    def _(act):
                        n_in = 0
                        for ch in range(CHUNKS):
                            def ask(fn):
                                nonlocal n_in
                                n_in += 1
                                act.wait_ge(act_in, n_in)
                                fn().then_inc(act_out, 1)
                            if kind == "gru":
                                ask(lambda: nc.scalar.activation(t1[:, :, 0:2 * FD], t1[:, :, 0:2 * FD], ACT.Sigmoid))
                                ask(lambda: nc.scalar.activation(t1[:, :, 2 * FD:3 * FD], t1[:, :, 2 * FD:3 * FD], ACT.Tanh))
                            if kind != "hidden":
                                ask(lambda: nc.scalar.activation(t1[:, :, 0:FD], y2[:, ch % 2], ACT.Square))
                                ask(lambda: nc.scalar.activation(small[:, 2, :], small[:, 1, :], ACT.Sqrt))
                            if not last:
                                for q, (k, b0, n) in enumerate(TP):
                                    act.wait_ge(turned, ch * len(TP) + q + 1)
                                    nc.scalar.copy(acc[:, k, (ch * CB + b0) * P:(ch * CB + b0 + n) * P],
                                                   pt[:, (ch * len(TP) + q) % 2, 0:n * P]).then_inc(turned_read, 1)

                    @block.sync
                    def _(sp):
                        for ch in range(CHUNKS):
                            js = slice(ch * CB, (ch + 1) * CB)
                            sp.wait_ge(rows_ready, ch + 1)
                            if not last:
                                sp.dma_start(table.rearrange("(b p) f -> p b f", p=P)[:, js, :], y2[:, ch % 2]
                                             ).then_inc(rows_out[ch % 2], 16)
                            elif ch < CHUNKS - 1:
                                sp.dma_start(out[ch * CB * P:(ch + 1) * CB * P, :].rearrange("(b p) f -> p b f", p=P),
                                             x[:, js, :]).then_inc(rows_out[ch % 2], 16)
                            else:
                                full = N // P
                                sp.dma_start(out[ch * CB * P:full * P, :].rearrange("(b p) f -> p b f", p=P),
                                             x[:, ch * CB:full, :]).then_inc(rows_out[ch % 2], 16)
                                sp.dma_start(out[full * P:N, :], x[0:N - full * P, full, :]).then_inc(rows_out[ch % 2], 16)
                        sp.wait_ge(rows_out[0], 16 * ((CHUNKS + 1) // 2 + last))
                        sp.wait_ge(rows_out[1], 16 * (CHUNKS // 2))

                    @block.vector
                    def _(dve):
                        chain = Chain(dve, d_dve)
                        n_ask = 0

                        def ask(ins):
                            nonlocal n_ask
                            n_ask += 1
                            ins.then_inc(act_in, 1)
                            dve.wait_ge(act_out, n_ask)

                        V = nc.vector
                        for ch in range(CHUNKS):
                            js = slice(ch * CB, (ch + 1) * CB)
                            xc = x[:, js, :]
                            y = y2[:, ch % 2]
                            if ch >= 2 and not last:
                                dve.wait_ge(rows_out[ch % 2], 16 * (ch // 2))
                                dve.wait_ge(turned, (ch - 1) * len(TP))
                            if ch and last:
                                dve.wait_ge(rows_ready, ch)
                            if kind == "gru":
                                for b in range(CB):
                                    n = ch * CB + b
                                    dve.wait_ge(conv_done, n + 1)
                                    V.scalar_tensor_tensor(out=t1[:, b, :], in0=bv[:], scalar=indeg[:, n:n + 1],
                                                           in1=po[:, n % nbuf, :], op0=ALU.mult, op1=ALU.add
                                                           ).then_inc(conv_read, 1)
                                dve.wait_ge(conv_read, (ch + 1) * CB)
                                r, z, i_n, h_n = (t1[:, :, q * FD:(q + 1) * FD] for q in range(4))
                                n_ask += 1
                                chain.step(V.tensor_copy(small[:, 0, :], dis_out[:, js]))
                                V.tensor_copy(small[:, 1, :], dis_out[:, js]).then_inc(act_in, 1)
                                dve.wait_ge(act_out, n_ask)
                                chain.step(V.tensor_tensor(h_n, h_n, r, ALU.mult))
                                ask(V.tensor_tensor(i_n, i_n, h_n, ALU.add))
                                chain.step(V.tensor_tensor(h_n, xc, i_n, ALU.subtract))
                                chain.step(V.tensor_tensor(h_n, h_n, z, ALU.mult))
                                chain.step(V.tensor_tensor(h_n, h_n, i_n, ALU.add))
                                chain.step(V.tensor_tensor(y, h_n, xc, ALU.add))
                            else:
                                dve.wait_ge(conv_done, ch + 1)
                                V.tensor_tensor(y, po[:, ch % nbuf, 0:CB * F].rearrange("p (b f) -> p b f", f=F),
                                                per_row(dis_in[:, js], F), ALU.mult).then_inc(conv_read, 1)
                                dve.wait_ge(conv_read, ch + 1)
                                chain.step(V.tensor_tensor(y, y, per_block(bias, CB), ALU.add))
                                if kind in ("relu", "hidden"):
                                    chain.step(V.tensor_scalar(y, y, 0.0, None, ALU.max))
                                if kind == "prelu":
                                    chain.step(V.tensor_scalar(t1[:], y, 0.0, prelu, ALU.min, ALU.mult))
                                    chain.step(V.scalar_tensor_tensor(out=y, in0=y, scalar=0.0, in1=t1[:],
                                                                      op0=ALU.max, op1=ALU.add))
                                if kind != "hidden":
                                    chain.step(V.tensor_tensor(y, y, xc, ALU.add))
                            if kind != "hidden":
                                s_sum, s_var, s_root, s_inv = (small[:, q, :] for q in range(4))
                                chain.step(V.tensor_reduce(s_sum, y, AX.X, ALU.add))
                                chain.step(V.tensor_scalar(s_sum, s_sum, 1.0 / FD, None, ALU.mult))
                                ask(V.tensor_tensor(y, y, per_row(s_sum, FD), ALU.subtract))
                                chain.step(V.tensor_reduce(s_var, t1[:, :, 0:FD], AX.X, ALU.add))
                                ask(V.tensor_scalar(s_var, s_var, 1.0 / FD, EPS, ALU.mult, ALU.add))
                                chain.step(V.reciprocal(s_inv, s_root))
                                norm = V.tensor_tensor(xc, y, per_row(s_inv, FD), ALU.mult)
                                if last:
                                    norm.then_inc(rows_ready, 1)
                                else:
                                    chain.step(norm)
                            if not last:
                                V.tensor_tensor(y, y if kind == "hidden" else xc, per_row(dis_out[:, js], F),
                                                ALU.mult).then_inc(rows_ready, 1)

        with ExitStack() as c:
            xT2 = sb("xT2", [P, NP], F32, c)
            sparse_pass("l0", p_table, FD, src_i, local, first_i, T, 8, W, messages=a["edge_feat"],
                        loads=[(xT2[:], a["x_feat"]), (x[:], a["x_nodes"])])
            gb = sb("gb", [1, 3 * FD], F32, c)
            again_in, gb_done = sem("again_in"), sem("gb_done")
            with nc.Block() as block:
                @block.sync
                def _(sp):
                    sp.dma_start(gru_bias[:, 0:3 * FD], a["bih"]).then_inc(again_in, 16)
                    sp.dma_start(gb[:], a["bhh"]).then_inc(again_in, 16)
                    sp.wait_ge(again_in, 32)

                @block.vector
                def _(dve):
                    dve.wait_ge(again_in, 32)
                    nc.vector.tensor_tensor(gru_bias[:, 0:2 * FD], gru_bias[:, 0:2 * FD], gb[:, 0:2 * FD],
                                            ALU.add).then_inc(gb_done, 1)
                    nc.vector.tensor_copy(gru_bias[:, 3 * FD:], gb[:, 2 * FD:]).then_inc(gb_done, 1)
                    dve.wait_ge(gb_done, 2)
            dense("l0", FD, None, "gru", None, None, dis1, tables[0], xT=xT2)

        with ExitStack() as c:
            rec_rows = sb("rec_rows", [P, GTR // P, P, 2], F32, c)
            ps_g = c.enter_context(nc.psum_tensor("ps_g", [P, 2, 1024], F32))
            rec_in, rec_turned, rec_read = sem("rec_in"), sem("rec_turned"), sem("rec_read")
            with nc.Block() as block:
                @block.sync
                def _(sp):
                    sp.dma_start(rec_rows[:].rearrange("p b e w -> p b (e w)"),
                                 groups.rearrange("(b p e) w -> p b (e w)", p=P, e=P)).then_inc(rec_in, 16)

                @block.tensor
                def _(pe):
                    pe.wait_ge(rec_in, 16)
                    for q in range(2):
                        for b in range(GTR // P):
                            mm = nc.tensor.transpose(ps_g[:, q, b * P:(b + 1) * P], rec_rows[:, b, :, q], ident[:])
                        mm.then_inc(rec_turned, 1)

                @block.vector
                def _(dve):
                    dve.wait_ge(rec_turned, 1)
                    nc.vector.tensor_copy(g_local[:], ps_g[:, 0, 0:GTR]).then_inc(rec_read, 1)
                    dve.wait_ge(rec_turned, 2)
                    nc.vector.tensor_copy(g_src_i[:], ps_g[:, 1, 0:GTR]).then_inc(rec_read, 1)
                    dve.wait_ge(rec_read, 2)

        sparse_pass("l1f", tables[0], FD, src_i, local, first_i, T, 16, W)
        sparse_pass("l1r", tables[0], FD, g_src_i, g_local, g_first_i, GT, 8, P, rounds=False)
        dense("l1", FD, [(l1w[:], 0)], "relu", dis1, l1b, dis2, tables[1])
        clear_sems()
        sparse_pass("l2", tables[1], FD, src_i, local, first_i, T, 16, W)
        dense("l2", FD, [(l2w[:], 0)], "prelu", dis2, l2b, dis3, tables[2])
        sparse_pass("l3a", tables[2], FD, src_i, local, first_i, T, 16, W, weights=weight)
        dense("l3a", HID, [(l3w1[:], 0)], "hidden", dis3, l3b1, dis3, h_tables[0])
        sparse_pass("l3b", h_tables[0], HID, src_i, local, first_i, T, 16, W, weights=weight)
        dense("l3b", HID, [(l3w2[:, k, :], k) for k in range(2)], "hidden", dis3, l3b2, dis3, h_tables[1])
        sparse_pass("l3c", h_tables[1], HID, src_i, local, first_i, T, 16, W, weights=weight)
        dense("l3c", FD, [(l3w3[:, k, :], k) for k in range(2)], "linear", dis3, l3b3, None, None, last=True)


def kernel(**inputs):
    import numpy as np
    import concourse.bacc as bacc
    from concourse.bass_utils import run_bass_kernel_spmd

    i = {k: np.asarray(v) for k, v in inputs.items()}

    def padded(v, n, fill):
        return np.concatenate([v, np.full((n - v.shape[0],) + v.shape[1:], fill, v.dtype)])

    def cols(v, fill):
        return padded(v, T * P, fill).reshape(T, P).T

    def rep(v, n=P):
        return np.broadcast_to(v[None, :], (n, v.shape[0]))

    x = padded(i["x"], NP, 0)
    w1 = i["L0_gnn_W1"]
    f = np.float32
    arrays = {
        "dst_rows": padded(i["dst"].astype(np.int32), TR * P, PAD_NODE).reshape(TR // P, P, P).transpose(1, 0, 2),
        "src_cols": cols(i["src"].astype(np.int32), PAD_NODE),
        "dst_cols": cols(i["dst"].astype(np.int32), PAD_NODE),
        "w_cols": cols(i["edge_weight"], 0),
        "edge_feat": np.concatenate([padded(i["edge_attr_64"], T * P, 0).T, np.ones((1, T * P), f)]),
        "x_nodes": x.reshape(NB, P, FD).transpose(1, 0, 2),
        "x_feat": x.T,
        "wihT": i["L0_gnn_Wih"].T,
        "whhT": i["L0_gnn_Whh"].T,
        "w2": i["L0_gnn_W2"],
        "b2r": np.broadcast_to(i["L0_gnn_b2"][:, None], (P, P)),
        "w1xT": w1[:, :FD].T,
        "w1eT": np.concatenate([w1[:, FD:].T, i["L0_gnn_b1"][None, :]]),
        "bih": i["L0_gnn_bih"][None, :],
        "bhh": i["L0_gnn_bhh"][None, :],
        "l1w": i["L1_gnn_W"].T,
        "l2w": i["L2_gnn_W"],
        "l3w1": i["L3_gnn_W1"],
        "l3w2": i["L3_gnn_W2"].reshape(2, P, HID).transpose(1, 0, 2),
        "l3w3": i["L3_gnn_W3"].reshape(2, P, FD).transpose(1, 0, 2),
        "biases": np.concatenate([rep(i[k]) for k in ("L1_gnn_bias", "L2_gnn_b", "L3_gnn_b3", "L3_gnn_b1",
                                                      "L3_gnn_b2", "L2_gnn_prelu_w")], axis=1),
    }
    nc = bacc.Bacc("TRN2", target_bir_lowering=False, num_devices=1)
    given, aps = {}, {}
    for name, v in arrays.items():
        v = np.ascontiguousarray(v)
        given[f"in_{name}"] = v
        aps[name] = nc.dram_tensor(f"in_{name}", v.shape, mybir.dt.from_np(v.dtype), kind="ExternalInput").ap()
    out = nc.dram_tensor("out", (N, FD), F32, kind="ExternalOutput").ap()
    build(nc, aps, out)
    r = run_bass_kernel_spmd(nc, [given], core_ids=[0])
    return r.results[0]["out"]
```
